# Optimizing a Trainium2 kernel written in Bass

```python
import numpy as np
import jax
import jax.numpy as jnp

def _softmax(x, axis=-1):
    return jax.nn.softmax(x, axis=axis)

def _gelu(x):
    return jax.nn.gelu(x, approximate=True)

def _silu(x):
    return jax.nn.silu(x)

def _sigmoid(x):
    return jax.nn.sigmoid(x)

def _layernorm(x, axis=-1, eps=1e-05):
    m = jnp.mean(x, axis=axis, keepdims=True)
    v = jnp.var(x, axis=axis, keepdims=True)
    return (x - m) / jnp.sqrt(v + eps)

def _scatter_add(tgt, idx, src, axis=0):
    return tgt.at[idx].add(src)

def _segment_sum(src, seg, n):
    return jax.ops.segment_sum(src, seg, n)
kernel_name = 'mk_gnn_preln_d1_gnn_r8_f757e2'

def setup_inputs(seed: int=0):
    np.random.seed(seed)
    _w = jnp.asarray

    def _rec_inputs():
        import jax
        import jax.numpy as jnp
        _gk = jax.random.key(seed)
        x = -0.0005121 + 1.001 * jax.random.normal(jax.random.fold_in(_gk, 1), (6250, 64), jnp.float32)
        src = jax.random.randint(jax.random.fold_in(_gk, 2), (200000,), 0, 6250, jnp.int32)
        dst = jax.random.randint(jax.random.fold_in(_gk, 3), (200000,), 0, 6250, jnp.int32)
        _o = jnp.argsort(dst, stable=True)
        src = src[_o]
        dst = dst[_o]
        node_vec = jax.random.uniform(jax.random.fold_in(_gk, 12), (6250,), jnp.float32, 0.0, 0.999957)
        return (x, src, dst, node_vec)
    x, src, dst, node_vec = _rec_inputs()

    def _L0_gnn_setup():
        import jax, jax.numpy as jnp
        import numpy as np
        N_NODES = 6250
        N_EDGES = 50000
        D_IN = 64
        D_OUT = 64
        G_HID = 128
        F_HID = 64
        HEADS = 4
        NEG_SLOPE = 0.2

        def _lrelu(v):
            return jnp.where(v >= 0, v, NEG_SLOPE * v)
        key = jax.random.key(seed)
        ks = jax.random.split(key, 8)
        x = jax.random.normal(ks[0], (N_NODES, D_IN), dtype=jnp.float32)
        edge_index = jax.random.randint(ks[1], (2, N_EDGES), 0, N_NODES, dtype=jnp.int64)
        pos = jax.random.uniform(ks[2], (N_NODES,), dtype=jnp.float32)
        s = 0.05
        gate_w1 = jax.random.normal(ks[3], (HEADS, F_HID, 2 * D_IN), dtype=jnp.float32) * s
        gate_w2 = jax.random.normal(ks[4], (HEADS, 1, F_HID), dtype=jnp.float32) * s
        msg_w1 = jax.random.normal(ks[5], (HEADS, G_HID, 2 * D_IN), dtype=jnp.float32) * s
        msg_w2 = jax.random.normal(ks[6], (HEADS, D_OUT, G_HID), dtype=jnp.float32) * s
        return {'x': x, 'edge_index': edge_index, 'pos': pos, 'gate_w1': gate_w1, 'gate_w2': gate_w2, 'msg_w1': msg_w1, 'msg_w2': msg_w2}
    _L0_gnn_all = _L0_gnn_setup()
    _L0_gnn_in = {k: v for k, v in _L0_gnn_all.items() if k in ('gate_w1', 'gate_w2', 'msg_w1', 'msg_w2')}
    del _L0_gnn_all
    return {'x': x, 'src': src, 'dst': dst, 'node_vec': node_vec, 'L0_gnn_gate_w1': _L0_gnn_in['gate_w1'], 'L0_gnn_gate_w2': _L0_gnn_in['gate_w2'], 'L0_gnn_msg_w1': _L0_gnn_in['msg_w1'], 'L0_gnn_msg_w2': _L0_gnn_in['msg_w2']}

def reference(x, src, dst, node_vec, L0_gnn_gate_w1, L0_gnn_gate_w2, L0_gnn_msg_w1, L0_gnn_msg_w2):
    import jax
    import jax.numpy as jnp

    def _L0_gnn_ref(x, edge_index, pos, gate_w1, gate_w2, msg_w1, msg_w2):
        import jax, jax.numpy as jnp
        import numpy as np
        N_NODES = 6250
        N_EDGES = 50000
        D_IN = 64
        D_OUT = 64
        G_HID = 128
        F_HID = 64
        HEADS = 4
        NEG_SLOPE = 0.2

        def _lrelu(v):
            return jnp.where(v >= 0, v, NEG_SLOPE * v)
        row, col = (edge_index[0], edge_index[1])
        e = jnp.concatenate([x[row], x[col]], axis=-1)
        g1 = _lrelu(jnp.einsum('ef,hgf->heg', e, gate_w1))
        alpha = _lrelu(jnp.einsum('heg,hog->heo', g1, gate_w2))
        w_edge = pos[col][None, :, None]
        a = w_edge * jnp.exp(alpha)
        seg = lambda t: jax.ops.segment_sum(t, row, num_segments=N_NODES)
        rowsum = jax.vmap(seg)(a)
        inv = 1.0 / rowsum + 1e-16
        alpha_n = a * inv[:, row]
        m1 = _lrelu(jnp.einsum('ef,hgf->heg', e, msg_w1))
        beta = _lrelu(jnp.einsum('heg,hog->heo', m1, msg_w2))
        out_h = jax.vmap(seg)(alpha_n * beta)
        return jnp.mean(out_h, axis=0)
    edge_index = jnp.stack([src, dst])
    h = jnp.maximum(_layernorm(x, axis=-1), 0.0)
    x = x + _L0_gnn_ref(h, edge_index, node_vec, L0_gnn_gate_w1, L0_gnn_gate_w2, L0_gnn_msg_w1, L0_gnn_msg_w2)
    return x

_drawn_inputs = setup_inputs


def setup_inputs(seed=0):
    import zlib

    import numpy as np

    out = dict(_drawn_inputs(seed))
    spreads = {}
    factors = {}
    for name, (base, spread) in spreads.items():
        noise = np.random.default_rng([zlib.crc32(name.encode()), seed]).standard_normal(out[name].shape)
        drawn = base * np.exp(spread * noise) if base else spread * noise
        out[name] = jnp.asarray(drawn.astype(out[name].dtype))
    for name, factor in factors.items():
        out[name] = (out[name] * factor).astype(out[name].dtype)
    return out
```

```python
from contextlib import ExitStack

import concourse.bass as bass
from concourse import mybir

F32 = mybir.dt.float32
F16 = mybir.dt.float16
BF16 = mybir.dt.bfloat16
I32 = mybir.dt.int32
ALU = mybir.AluOpType
ACT = mybir.ActivationFunctionType
AX = mybir.AxisListType
RMAX = bass.bass_isa.ReduceOp.max

P = 128
NEG_SLOPE = 0.2
EPS = 1e-5
GROUP = 256
TILES = GROUP // P
SLOTS = 4
BATCH = 8
H_SCALE = 256.0
PAD_KEY = 255


def gnn_preln_kernel(nc, x, src, dst, node_vec, gate_w1, gate_w2, msg_w1, msg_w2, out):
    N, D = x.shape
    E = src.shape[0]
    HEADS, G_HID, _ = msg_w1.shape
    F_HID = gate_w1.shape[1]
    assert D == 64 and G_HID == P and F_HID == 64 and HEADS == 4

    BLOCKS = -(-N // P)
    LAST = N - (BLOCKS - 1) * P
    BUCKETS = BLOCKS + 1
    NJ = -(-E // P)
    NJ += -NJ % (2 * BATCH)
    FULL = E // NJ
    REST = E - FULL * NJ
    GROUPS = (P * NJ + BUCKETS * (GROUP - 1)) // GROUP
    GROUPS += -GROUPS % SLOTS
    BODIES = GROUPS // SLOTS
    T = GROUPS * TILES
    TC = -(-T // P)
    HID_CHUNKS = (HEADS * F_HID + HEADS * G_HID) // P
    PAIRS = HID_CHUNKS // 2
    VALS = HEADS * D
    VROW = VALS + HEADS + 1
    HROW = D + 1
    assert FULL == P - 1 and BUCKETS <= F_HID and D * 2 == P

    key_d = nc.dram_tensor("key_d", [P, T], I32).ap()
    key_flat = key_d.rearrange("p (t o) -> (p t) o", o=1)
    place_d = nc.dram_tensor("place_d", [TC * P, P], BF16).ap()
    place_flat = place_d.rearrange("t p -> (t p)")
    node_d = nc.dram_tensor("node_d", [BUCKETS * P, HROW], F32).ap()

    with ExitStack() as ctx:
        def sb(name, shape, dt):
            return ctx.enter_context(nc.sbuf_tensor(name, shape, dt))

        def ps(name, shape, dt=F32):
            return ctx.enter_context(nc.psum_tensor(name, shape, dt))

        def sem(name):
            return ctx.enter_context(nc.semaphore(name))

        ident = sb("ident", [P, P], F32)
        ident_h = sb("ident_h", [P, P], F16)
        ident_b = sb("ident_b", [P, P], BF16)
        before = sb("before", [P, P], F32)
        real = sb("real", [P, P], F32)
        ones = sb("ones", [P, P], F32)
        iota_row = sb("iota_row", [P, P], F32)
        iota_col = sb("iota_col", [P, 1], F32)
        iota_group = sb("iota_group", [P, GROUPS], F32)
        xs = sb("xs", [P, BLOCKS, D], F32)
        xc = sb("xc", [P, BLOCKS, D], F32)
        h32 = sb("h32", [P, BLOCKS, D], F32)
        node = sb("node", [P, BUCKETS, HROW], F32)
        node_h = node[:, 0:BLOCKS, 0:D].bitcast(F16)
        stat = sb("stat", [P, 6, BLOCKS], F32)
        pos_rows = sb("pos_rows", [64, P], F32)
        w1 = sb("w1", [P, HID_CHUNKS, P], F32)
        w1t = sb("w1t", [P, HID_CHUNKS, P], F32)
        w1_hi = sb("w1_hi", [P, HID_CHUNKS, P], F16)
        w1_lo = sb("w1_lo", [P, HID_CHUNKS, P], F16)
        w2 = sb("w2", [P, 2, P], F32)
        w2t = sb("w2t", [P, HEADS, D], F32)
        gw2 = sb("gw2", [P, 2, HEADS], F32)
        gw2s = sb("gw2s", [P, 2, HEADS], F32)
        wmax = sb("wmax", [P, 6], F32)
        wexp = sb("wexp", [P, 3], I32)
        acc = sb("acc", [P, BUCKETS, VROW], F32)
        work = acc[:, :, :].rearrange("p b r -> p (b r)")[:, 0:8 * NJ].rearrange("p (k j) -> p k j", j=NJ)
        src_i, blk_i, rank_p, rank_t = (work[:, k, :].bitcast(I32) for k in range(4))
        cum, rank, picked = work[:, 4, :], work[:, 5, :], work[:, 6:8, :]
        dst_i = sb("dst_i", [P, NJ], I32)
        blk_b = sb("blk_b", [P, NJ], BF16)
        ones_b = sb("ones_b", [P, NJ], BF16)
        sign_out = sb("sign_out", [P, NJ], BF16)
        bias = sb("bias", [P, 1], F32)
        sign_sum = sb("sign_sum", [P, BUCKETS + 1], F32)
        count = sb("count", [P, BUCKETS], F32)
        tot = sb("tot", [P, BUCKETS], F32)
        grp_i = sb("grp_i", [P, BUCKETS], I32)
        grp = sb("grp", [P, BUCKETS], F32)
        cum_grp = sb("cum_grp", [P, BUCKETS], F32)
        start = sb("start", [P, BUCKETS], F32)
        end_col = sb("end_col", [P, 1], F32)
        tmp_b = sb("tmp_b", [P, BUCKETS], F32)
        blk_row = sb("blk_row", [P, GROUPS], I32)
        bucket = sb("bucket", [P, 1], F32)
        first = sb("first", [P, 1], F32)
        mask = sb("mask", [P, NJ], BF16)
        rank_i = sb("rank_i", [P, NJ], I32)
        stage_key = sb("stage_key", [P, 2, BATCH], I32)
        stage_addr = sb("stage_addr", [P, 2, BATCH], I32)
        skey = sb("skey", [P, T], I32)
        sdst = sb("sdst", [P, T], I32)
        splace = sb("splace", [P, T], F32)
        splace_b = sb("splace_b", [P, TC * P], BF16)
        place_t = sb("place_t", [P, TC, P], BF16)
        idx = sb("idx", [P, SLOTS, TILES], I32)
        rows = sb("rows", [P, SLOTS, TILES, HROW], F32)
        place_bc = sb("place_bc", [P, SLOTS, GROUP], BF16)
        hblk = sb("hblk", [P, SLOTS, D], F32)
        pick = sb("pick", [P, 2, GROUP], F16)
        feat = sb("feat", [P, 2, GROUP], F16)
        hidden = sb("hidden", [P, PAIRS, 2, GROUP], F32)
        alpha = sb("alpha", [P, 2, TILES, HEADS], F32)
        expa = sb("expa", [P, 2, TILES, HEADS], F32)
        hid_s = sb("hid_s", [P, PAIRS, 2, GROUP], F32)
        alpha_s = sb("alpha_s", [P, TILES, HEADS], F32)
        beta_s = sb("beta_s", [P, TILES, VALS], F32)
        beta = sb("beta", [P, TILES, VALS], F32)
        vals = sb("vals", [P, 2, TILES, VROW], F32)
        leave = sb("leave", [P, 2, TILES, P], F32)
        inv = sb("inv", [P, 3, BLOCKS, HEADS], F32)
        empty = sb("empty", [P, BLOCKS], F32)

        ps_a = [ps(f"ps_a{c}", [P, 2, GROUP]) for c in range(PAIRS)]
        ps_x = ps("ps_x", [P, 2, GROUP])
        ps_b = ps("ps_b", [P, TILES, VALS])
        ps_g = ps("ps_g", [P, 512])[:, 0:TILES * HEADS].rearrange("p (t h) -> p t h", h=HEADS)
        ps_s = ps("ps_s", [P, 512])[:, 0:VROW]
        ps_t = ps("ps_t", [P, 8, P], BF16)

        ps_pos = ps_b[:, :, :].rearrange("p t v -> p (t v)")[:, 0:64]
        ps_a_flat = [ps_a[c][:, :, :].rearrange("p a g -> p (a g)") for c in range(PAIRS)]
        ps_w = [ps_a[c][:, 0, :].rearrange("p (a e) -> p a e", a=2) for c in range(PAIRS)]

        s_const = sem("s_const")
        s_pre = sem("s_pre")
        s_xin = sem("s_xin")
        s_win = sem("s_win")
        s_ein = sem("s_ein")
        s_pad = sem("s_pad")
        s_v = sem("s_v")
        s_var = sem("s_var")
        s_std = sem("s_std")
        s_wt = sem("s_wt")
        s_wmax = sem("s_wmax")
        s_wmaxa = sem("s_wmaxa")
        s_wcopy = sem("s_wcopy")
        s_node = sem("s_node")
        s_nout = sem("s_nout")
        s_blk = sem("s_blk")
        s_bias = sem("s_bias")
        s_sign = sem("s_sign")
        s_count = sem("s_count")
        s_pref = sem("s_pref")
        s_past = sem("s_past")
        s_blkp = sem("s_blkp")
        s_blkrow = sem("s_blkrow")
        s_first = sem("s_first")
        s_mask = sem("s_mask")
        s_cum = sem("s_cum")
        s_picked = sem("s_picked")
        s_rank = sem("s_rank")
        s_addr = sem("s_addr")
        s_staged = sem("s_staged")
        s_seen = sem("s_seen")
        s_scat = [sem(f"s_scat{u}") for u in range(2)]
        s_skey = sem("s_skey")
        s_place = sem("s_place")
        s_pt = sem("s_pt")
        s_ptc = sem("s_ptc")
        s_pout = sem("s_pout")
        s_idx = sem("s_idx")
        s_rows = [sem(f"s_rows{u}") for u in range(SLOTS)]
        s_in = [sem(f"s_in{u}") for u in range(SLOTS)]
        s_pick = sem("s_pick")
        s_x = sem("s_x")
        s_feat = sem("s_feat")
        s_l1 = sem("s_l1")
        s_hid = sem("s_hid")
        s_gate = sem("s_gate")
        s_hids = sem("s_hids")
        s_alphas = sem("s_alphas")
        s_betas = sem("s_betas")
        s_alpha = sem("s_alpha")
        s_expa = sem("s_expa")
        s_l2 = sem("s_l2")
        s_beta = sem("s_beta")
        s_wgt = sem("s_wgt")
        s_vals = sem("s_vals")
        s_leave = sem("s_leave")
        s_seg = sem("s_seg")
        s_acc = sem("s_acc")
        s_clear = sem("s_clear")
        s_final = sem("s_final")
        s_out = sem("s_out")

        block = ctx.enter_context(nc.Block())

        N_CONST = 11
        N_XIN = 4
        N_WIN = 6

        @block.sync
        def _(sp):
            sp.wait_ge(s_pre, 5)
            sp.dma_start(src_i[0:FULL, :], src[0:FULL * NJ].rearrange("(p j) -> p j", j=NJ)).then_inc(s_ein, 16)
            sp.dma_start(src_i[FULL:FULL + 1, 0:REST], src[FULL * NJ:E].rearrange("(p j) -> p j", p=1)).then_inc(s_ein, 16)
            sp.dma_start(dst_i[0:FULL, :], dst[0:FULL * NJ].rearrange("(p j) -> p j", j=NJ)).then_inc(s_ein, 16)
            sp.dma_start(dst_i[FULL:FULL + 1, 0:REST], dst[FULL * NJ:E].rearrange("(p j) -> p j", p=1)).then_inc(s_ein, 16)
            sp.dma_start(xs[:, 0:BLOCKS - 1, :],
                         x[0:(BLOCKS - 1) * P, :].rearrange("(b p) d -> p b d", p=P)).then_inc(s_xin, 16)
            sp.dma_start(xs[0:LAST, BLOCKS - 1, :], x[(BLOCKS - 1) * P:N, :]).then_inc(s_xin, 16)
            sp.dma_start(pos_rows[0:BLOCKS - 1, :],
                         node_vec[0:(BLOCKS - 1) * P].rearrange("(b p) -> b p", p=P)).then_inc(s_xin, 16)
            sp.dma_start(pos_rows[BLOCKS - 1:BLOCKS, 0:LAST],
                         node_vec[(BLOCKS - 1) * P:N].rearrange("(b p) -> b p", b=1)).then_inc(s_xin, 16)
            sp.dma_start(w1[:, 0:2, :], gate_w1.rearrange("(c a) f e -> (a f) c e", a=2)).then_inc(s_win, 16)
            sp.dma_start(w1[:, 2:2 + HEADS, :], msg_w1.rearrange("h f e -> f h e")).then_inc(s_win, 16)
            for h in range(HEADS):
                sp.dma_start(w2[(h % 2) * D:(h % 2 + 1) * D, h // 2, :], msg_w2[h, :, :]).then_inc(s_win, 16)
            sp.dma_start(key_d, skey[:, :]).then_inc(s_pad, 16)
            sp.wait_ge(s_node, 1)
            sp.dma_start(node_d.rearrange("(b p) r -> p b r", p=P), node[:, :, :]).then_inc(s_nout, 16)
            for u in range(2):
                sp.wait_ge(s_scat[u], 16 * NJ // 2)
            sp.dma_start(skey[:, :], key_d).then_inc(s_skey, 16)
            sp.wait_ge(s_ptc, 2)
            sp.dma_start(place_d.rearrange("(a t) p -> t a p", t=P), place_t[:, :, :]).then_inc(s_pout, 16)
            sp.wait_ge(s_pout, 16)
            sp.wait_ge(s_nout, 16)
            sp.wait_ge(s_blkrow, 1)

            def load(g, i, u):
                blk = sp.value_load(blk_row[0:1, bass.ds(g, 1)], min_val=0, max_val=BLOCKS)
                if i is not None:
                    sp.wait_ge(s_x, SLOTS * i + u - SLOTS + 1)
                    sp.wait_ge(s_pick, SLOTS * i + u - SLOTS + 1)
                sp.dma_start(hblk[:, u, :], node_d[bass.ds(blk * P, P), 0:D]).then_inc(s_in[u], 16)
                sp.dma_start(place_bc[:, u, :],
                             place_flat[bass.ds(g * GROUP, GROUP)].rearrange("(o n) -> o n", o=1)
                             .to_broadcast([P, GROUP])).then_inc(s_in[u], 16)

            for u in range(SLOTS):
                load(u, None, u)
            with sp.Fori(1, BODIES) as i:
                for u in range(SLOTS):
                    load(i * SLOTS + u, i, u)
            sp.wait_ge(s_final, 1)
            sp.dma_start(out[0:(BLOCKS - 1) * P, :].rearrange("(b p) d -> p b d", p=P),
                         h32[:, 0:BLOCKS - 1, :]).then_inc(s_out, 16)
            sp.dma_start(out[(BLOCKS - 1) * P:N, :], h32[0:LAST, BLOCKS - 1, :]).then_inc(s_out, 16)
            sp.wait_ge(s_out, 32)

        @block.gpsimd
        def _(pool):
            pool.memset(ident[:, :], 0.0).then_inc(s_const, 1)
            pool.memset(ones[:, :], 1.0).then_inc(s_const, 1)
            pool.iota(iota_row[:, :], pattern=[[1, P]], base=0, channel_multiplier=0,
                      allow_small_or_imprecise_dtypes=True).then_inc(s_const, 1)
            pool.iota(iota_col[:, :], pattern=[[1, 1]], base=0, channel_multiplier=1,
                      allow_small_or_imprecise_dtypes=True).then_inc(s_const, 1)
            pool.iota(iota_group[:, :], pattern=[[1, GROUPS]], base=0, channel_multiplier=0,
                      allow_small_or_imprecise_dtypes=True).then_inc(s_const, 1)
            pool.wait_ge(s_const, 5)
            pool.affine_select(out=ident[:, :], in_=ident[:, :], compare_op=ALU.not_equal, fill=1.0,
                               base=0, pattern=[[-1, P]], channel_multiplier=1).then_inc(s_const, 1)
            pool.affine_select(out=before[:, :], in_=ones[:, :], compare_op=ALU.is_gt, fill=0.0,
                               base=0, pattern=[[1, P]], channel_multiplier=-1).then_inc(s_const, 1)
            pool.affine_select(out=real[:, :], in_=ones[:, :], compare_op=ALU.is_gt, fill=0.0,
                               base=BLOCKS, pattern=[[0, P]], channel_multiplier=-1).then_inc(s_const, 1)
            pool.wait_ge(s_const, 8)
            pool.tensor_copy(ident_h[:, :], ident[:, :]).then_inc(s_const, 1)
            pool.tensor_copy(ident_b[:, :], ident[:, :]).then_inc(s_const, 1)
            pool.memset(rank[:, :], 0.0).then_inc(s_const, 1)
            pool.wait_ge(s_wmax, 1)
            pool.partition_all_reduce(wmax[:, 1:2], wmax[:, 0:1], P, RMAX).then_inc(s_wmaxa, 1)
            pool.wait_ge(s_const, N_CONST)
            pool.wait_ge(s_picked, 1)
            pool.tensor_tensor(rank[:, :], rank[:, :], picked[:, 0, :], ALU.add).then_inc(s_rank, 1)
            pool.wait_ge(s_picked, 2)
            pool.wait_ge(s_rank, 1)
            pool.tensor_tensor(rank[:, :], rank[:, :], picked[:, 1, :], ALU.add).then_inc(s_rank, 1)
            with pool.Fori(1, BUCKETS // 2) as b2:
                for u in range(2):
                    pool.wait_ge(s_picked, b2 * 2 + u + 1)
                    pool.wait_ge(s_rank, b2 * 2 + u)
                    pool.tensor_tensor(rank[:, :], rank[:, :], picked[:, u, :], ALU.add).then_inc(s_rank, 1)

            pool.wait_ge(s_pad, 16)

            def scatter(staged, u):
                pool.wait_ge(s_staged, staged)
                pool.sem_inc(s_seen, 1)
                for k in range(BATCH):
                    pool.indirect_dma_start(
                        out=key_flat, out_offset=bass.IndirectOffsetOnAxis(ap=stage_addr[:, u, k:k + 1], axis=0),
                        in_=stage_key[:, u, k:k + 1], in_offset=None).then_inc(s_scat[u], 16)

            with pool.Fori(0, NJ // (2 * BATCH)) as j:
                for u in range(2):
                    scatter(j * 4 + (2 * u + 2), u)

            pool.wait_ge(s_place, 1)
            pool.wait_ge(s_nout, 16)

            def gather(g, i, u):
                if i is not None:
                    pool.wait_ge(s_rows[u], i * 32)
                    pool.wait_ge(s_x, SLOTS * i + u - SLOTS + 1)
                    pool.wait_ge(s_wgt, SLOTS * i + u - SLOTS + 1)
                    pool.sem_inc(s_seen, 1)
                pool.tensor_copy(idx[:, u, :], sdst[:, bass.ds(g * TILES, TILES)]).then_inc(s_idx, 1)
                pool.wait_ge(s_idx, g + 1)
                pool.sem_inc(s_seen, 1)
                for t in range(TILES):
                    pool.indirect_dma_start(
                        out=rows[:, u, t, :], out_offset=None, in_=node_d,
                        in_offset=bass.IndirectOffsetOnAxis(ap=idx[:, u, t:t + 1], axis=0)).then_inc(s_rows[u], 16)

            for u in range(SLOTS):
                gather(u, None, u)
            with pool.Fori(1, BODIES) as i:
                for u in range(SLOTS):
                    gather(i * SLOTS + u, i, u)

        @block.scalar
        def _(act):
            act.wait_ge(s_pre, 5)
            for h in range(HEADS):
                act.dma_start(gw2[(h % 2) * F_HID:(h % 2 + 1) * F_HID, h // 2, h:h + 1],
                              gate_w2[h, :, :].rearrange("o f -> f o")).then_inc(s_win, 16)
            act.wait_ge(s_var, 1)
            act.activation(stat[:, 3, :], stat[:, 2, :], ACT.Sqrt).then_inc(s_std, 1)
            act.wait_ge(s_blk, 1)
            act.activation(sign_out[:, :], blk_b[:, :], ACT.Sign, bias=bias[:, 0:1],
                           accum_out=sign_sum[:, 0:1]).then_inc(s_sign, 1)
            with act.Fori(1, BUCKETS) as b:
                act.wait_ge(s_sign, b)
                act.activation(bias[:, :], bias[:, :], ACT.Copy, bias=-1.0).then_inc(s_bias, 1)
                act.wait_ge(s_bias, b)
                act.activation(sign_out[:, :], blk_b[:, :], ACT.Sign, bias=bias[:, 0:1],
                               accum_out=sign_sum[:, bass.ds(b, 1)]).then_inc(s_sign, 1)

            def scaled(g, c):
                act.wait_ge(s_l1, g * PAIRS + c + 1)
                if not (isinstance(g, int) and g < 1):
                    act.wait_ge(s_hid, g * PAIRS + (c - PAIRS + 1))
                act.activation(hid_s[:, c, :, :], ps_a[c][:, :, :], ACT.Copy, scale=NEG_SLOPE).then_inc(s_hids, 1)

            def copy_feat(g):
                act.wait_ge(s_x, g + 1)
                act.activation(feat[:, :, :], ps_x[:, :, :], ACT.Copy).then_inc(s_feat, 1)

            def step(g, s, last=False):
                early = isinstance(g, int) and g < 2
                for c in range(PAIRS):
                    scaled(g, c)
                if not last:
                    copy_feat(g + 1)
                act.wait_ge(s_gate, g + 1)
                if not (isinstance(g, int) and g < 1):
                    act.wait_ge(s_alpha, g)
                act.activation(alpha_s[:, :, :], ps_g[:, :, :], ACT.Copy, scale=NEG_SLOPE).then_inc(s_alphas, 1)
                act.wait_ge(s_alpha, g + 1)
                if not early:
                    act.wait_ge(s_wgt, g - 1)
                act.activation(expa[:, s, :, :], alpha[:, s, :, :], ACT.Exp).then_inc(s_expa, 1)
                act.wait_ge(s_l2, g + 1)
                if not (isinstance(g, int) and g < 1):
                    act.wait_ge(s_beta, g)
                act.activation(beta_s[:, :, :], ps_b[:, :, :], ACT.Copy, scale=NEG_SLOPE).then_inc(s_betas, 1)

            copy_feat(0)
            for u in range(SLOTS):
                step(u, u % 2)
            with act.Fori(1, BODIES - 1) as i:
                for u in range(SLOTS):
                    step(i * SLOTS + u, u % 2)
            for u in range(SLOTS):
                step((BODIES - 1) * SLOTS + u, u % 2, last=u == SLOTS - 1)

        @block.vector
        def _(dve):
            chain = [0]

            def link(ins):
                chain[0] += 1
                ins.then_inc(s_v, 1)
                dve.wait_ge(s_v, chain[0])

            dve.memset(src_i[96:P, :], BLOCKS * P).then_inc(s_pre, 1)
            dve.memset(dst_i[96:P, :], 0).then_inc(s_pre, 1)
            dve.memset(xs[:, BLOCKS - 1, :], 0.0).then_inc(s_pre, 1)
            dve.memset(gw2[:, :, :], 0.0)
            dve.memset(pos_rows[:, :], 0.0).then_inc(s_pre, 1)
            dve.memset(skey[:, :], PAD_KEY).then_inc(s_pre, 1)
            dve.memset(ones_b[:, :], 1.0)
            dve.memset(vals[:, :, :, VROW - 1:VROW], 1.0)
            dve.memset(splace_b[:, T:TC * P], float(PAD_KEY))
            link(dve.memset(node[:, :, :], 0.0))

            dve.memset(bias[:, :], 0.5)
            dve.memset(bucket[:, :], 0.0)
            dve.wait_ge(s_ein, 64)
            link(dve.tensor_scalar(blk_i[:, :], src_i[:, :], 7, None, ALU.logical_shift_right))
            dve.tensor_copy(blk_b[:, :], blk_i[:, :]).then_inc(s_blk, 1)
            link(dve.tensor_scalar(rank_i[:, :], src_i[:, :], P - 1, None, ALU.bitwise_and))
            link(dve.scalar_tensor_tensor(dst_i[:, :], dst_i[:, :], 256.0, rank_i[:, :], ALU.mult, ALU.add))

            dve.wait_ge(s_xin, 16 * N_XIN)
            link(dve.tensor_reduce(stat[:, 0, :], xs[:, :, :], AX.X, ALU.add))
            link(dve.tensor_scalar(stat[:, 1, :], stat[:, 0, :], 1.0 / D, None, ALU.mult))
            link(dve.tensor_tensor(xc[:, :, :], xs[:, :, :],
                                   stat[:, 1, :].unsqueeze(2).to_broadcast([P, BLOCKS, D]), ALU.subtract))
            link(dve.tensor_tensor(h32[:, :, :], xc[:, :, :], xc[:, :, :], ALU.mult))
            link(dve.tensor_reduce(stat[:, 0, :], h32[:, :, :], AX.X, ALU.add))
            dve.tensor_scalar(stat[:, 2, :], stat[:, 0, :], 1.0 / D, EPS, ALU.mult, ALU.add).then_inc(s_var, 1)
            dve.wait_ge(s_std, 1)
            link(dve.reciprocal(stat[:, 4, :], stat[:, 3, :]))
            link(dve.tensor_scalar(stat[:, 5, :], stat[:, 4, :], H_SCALE, None, ALU.mult))
            link(dve.tensor_tensor(xc[:, :, :], xc[:, :, :],
                                   stat[:, 5, :].unsqueeze(2).to_broadcast([P, BLOCKS, D]), ALU.mult))
            link(dve.tensor_scalar(h32[:, :, :], xc[:, :, :], 0.0, None, ALU.max))
            link(dve.tensor_copy(node_h[:, :, 0:D], h32[:, :, :]))
            link(dve.tensor_tensor(node_h[:, :, D:2 * D], h32[:, :, :], node_h[:, :, 0:D], ALU.subtract))
            dve.wait_ge(s_wt, 1)
            dve.tensor_copy(node[:, 0:BLOCKS, D:HROW].rearrange("p b o -> p (b o)"),
                            ps_pos[:, 0:BLOCKS]).then_inc(s_node, 1)

            dve.wait_ge(s_win, 16 * (N_WIN + HEADS))
            link(dve.tensor_reduce(wmax[:, 2:3], w1[:, :, :].rearrange("p c e -> p (c e)"), AX.X, ALU.max))
            link(dve.tensor_reduce(wmax[:, 3:4], w1[:, :, :].rearrange("p c e -> p (c e)"), AX.X, ALU.min))
            link(dve.tensor_scalar(wmax[:, 4:5], wmax[:, 3:4], -1.0, 1e-30, ALU.mult, ALU.max))
            dve.tensor_tensor(wmax[:, 0:1], wmax[:, 2:3], wmax[:, 4:5], ALU.max).then_inc(s_wmax, 1)
            dve.wait_ge(s_wmaxa, 1)
            link(dve.tensor_scalar(wexp[:, 0:1], wmax[:, 1:2].bitcast(I32), 23, None, ALU.logical_shift_right))
            link(dve.tensor_scalar(wexp[:, 1:2], wexp[:, 0:1], -1.0, 264.0, ALU.mult, ALU.add))
            link(dve.tensor_scalar(wexp[:, 2:3], wexp[:, 0:1], -10.0, None, ALU.add))
            link(dve.tensor_scalar(wexp[:, 1:3], wexp[:, 1:3], 23, None, ALU.logical_shift_left))
            scale = wexp[:, 1:2].bitcast(F32)
            unscale = wexp[:, 2:3].bitcast(F32)
            for c in range(PAIRS):
                dve.wait_ge(s_wt, 2 + c)
                link(dve.tensor_scalar(w1t[:, 2 * c:2 * c + 2, :], ps_w[c], scale, None, ALU.mult))
            link(dve.tensor_copy(w1_hi[:, :, :], w1t[:, :, :]))
            link(dve.tensor_tensor(w1_lo[:, :, :], w1t[:, :, :], w1_hi[:, :, :], ALU.subtract))
            dve.wait_ge(s_wt, 5)
            link(dve.tensor_scalar(w2t[:, :, :], ps_x[:, 0, :].rearrange("p (h d) -> p h d", d=D),
                                   unscale, 1.0 / H_SCALE, ALU.mult, ALU.mult))
            dve.tensor_scalar(gw2s[:, :, :], gw2[:, :, :], unscale, 1.0 / H_SCALE,
                              ALU.mult, ALU.mult).then_inc(s_wcopy, 1)

            dve.wait_ge(s_sign, BUCKETS)
            link(dve.memset(sign_sum[:, BUCKETS:BUCKETS + 1], -float(NJ)))
            link(dve.tensor_tensor(count[:, :], sign_sum[:, 0:BUCKETS], sign_sum[:, 1:BUCKETS + 1], ALU.subtract))
            dve.tensor_scalar(count[:, :], count[:, :], 0.5, None, ALU.mult).then_inc(s_count, 1)
            dve.wait_ge(s_pref, 1)
            link(dve.tensor_scalar(grp_i[:, :], ps_s[:, BUCKETS:2 * BUCKETS], float(GROUP - 1), None, ALU.add))
            link(dve.tensor_scalar(grp_i[:, :], grp_i[:, :], GROUP.bit_length() - 1, None, ALU.logical_shift_right))
            link(dve.tensor_copy(grp[:, :], grp_i[:, :]))
            link(dve.tensor_tensor_scan(cum_grp[:, :], ones[:, 0:BUCKETS], grp[:, :], 0.0, ALU.mult, ALU.add))
            link(dve.tensor_tensor(tmp_b[:, :], cum_grp[:, :], grp[:, :], ALU.subtract))
            link(dve.scalar_tensor_tensor(start[:, :], tmp_b[:, :], float(GROUP), ps_s[:, 0:BUCKETS], ALU.mult, ALU.add))
            link(dve.tensor_scalar(start[:, :], start[:, :], -1.0, None, ALU.add))
            link(dve.tensor_tensor(tmp_b[:, :], cum_grp[:, :], ident[:, 0:BUCKETS], ALU.mult))
            link(dve.tensor_reduce(end_col[:, :], tmp_b[:, :], AX.X, ALU.add))
            dve.tensor_scalar(iota_group[:, :], iota_group[:, :], end_col[:, 0:1], None, ALU.is_ge).then_inc(s_past, 1)
            dve.wait_ge(s_blkp, 1)
            dve.tensor_copy(blk_row[:, 0:GROUPS // 2], ps_a_flat[0][:, 0:GROUPS // 2])
            dve.tensor_copy(blk_row[:, GROUPS // 2:GROUPS], ps_a_flat[1][:, 0:GROUPS // 2]).then_inc(s_blkrow, 1)

            def bucket_places(b, u):
                dve.tensor_copy(first[:, :], start[:, bass.ds(b, 1)]).then_inc(s_first, 1)
                dve.tensor_scalar(mask[:, :], blk_b[:, :], bucket[:, 0:1], None, ALU.is_equal).then_inc(s_mask, 1)
                dve.wait_ge(s_mask, b + 1)
                dve.wait_ge(s_first, 2 * b + 1)
                dve.tensor_tensor_scan(cum[:, :], ones_b[:, :], mask[:, :], first[:, 0:1],
                                       ALU.mult, ALU.add).then_inc(s_cum, 1)
                dve.tensor_scalar(bucket[:, :], bucket[:, :], 1.0, None, ALU.add).then_inc(s_first, 1)
                dve.wait_ge(s_cum, b + 1)
                if not isinstance(b, int):
                    dve.wait_ge(s_rank, b - 1)
                dve.tensor_tensor(picked[:, u, :], cum[:, :], mask[:, :], ALU.mult).then_inc(s_picked, 1)
                dve.wait_ge(s_picked, b + 1)
                dve.wait_ge(s_first, 2 * b + 2)

            for u in range(2):
                bucket_places(u, u)
            with dve.Fori(1, BUCKETS // 2) as b2:
                for u in range(2):
                    bucket_places(b2 * 2 + u, u)

            dve.wait_ge(s_rank, BUCKETS)
            link(dve.tensor_copy(rank_i[:, :], rank[:, :]))
            dve.tensor_scalar(rank_p[:, :], rank_i[:, :], P - 1, None, ALU.bitwise_and)
            link(dve.tensor_scalar(rank_t[:, :], rank_i[:, :], 7, None, ALU.logical_shift_right))
            link(dve.scalar_tensor_tensor(rank_i[:, :], rank_p[:, :], float(T), rank_t[:, :], ALU.mult, ALU.add))

            dve.memset(acc[:, :, :], 0.0).then_inc(s_clear, 1)

            def stage(j, u):
                dve.tensor_copy(stage_addr[:, u, :], rank_i[:, bass.ds(j, BATCH)]).then_inc(s_staged, 1)
                dve.tensor_copy(stage_key[:, u, :], dst_i[:, bass.ds(j, BATCH)]).then_inc(s_staged, 1)

            for u in range(2):
                stage(u * BATCH, u)
            with dve.Fori(1, NJ // (2 * BATCH)) as j:
                for u in range(2):
                    dve.wait_ge(s_scat[u], j * (16 * BATCH))
                    stage(j * (2 * BATCH) + u * BATCH, u)

            dve.wait_ge(s_skey, 16)
            dve.tensor_scalar(sdst[:, :], skey[:, :], 8, None, ALU.logical_shift_right).then_inc(s_place, 1)
            link(dve.tensor_scalar(skey[:, :], skey[:, :], 255, None, ALU.bitwise_and))
            dve.tensor_copy(splace[:, :], skey[:, :])
            dve.tensor_copy(splace_b[:, 0:T], skey[:, :]).then_inc(s_place, 1)
            dve.wait_ge(s_pt, 1)
            dve.tensor_copy(place_t[:, 0:8, :], ps_t[:, :, :]).then_inc(s_ptc, 1)
            dve.wait_ge(s_pt, 2)
            dve.tensor_copy(place_t[:, 8:TC, :], ps_t[:, 0:TC - 8, :]).then_inc(s_ptc, 1)

            def compare(g, i, u):
                dve.wait_ge(s_in[u], (i + 1) * 32)
                if not (isinstance(g, int) and g < 2):
                    dve.wait_ge(s_x, g - 1)
                dve.tensor_scalar(pick[:, u % 2, :], place_bc[:, u, :], iota_col[:, 0:1], None,
                                  ALU.is_equal).then_inc(s_pick, 1)

            def leaky(g, c):
                dve.wait_ge(s_hids, g * PAIRS + c + 1)
                dve.tensor_tensor(hidden[:, c, :, :], ps_a[c][:, :, :], hid_s[:, c, :, :], ALU.max).then_inc(s_hid, 1)

            def add_up(g, blk):
                dve.wait_ge(s_seg, g + 1)
                if isinstance(g, int) and g < 1:
                    dve.wait_ge(s_clear, 1)
                else:
                    dve.wait_ge(s_acc, g)
                row = acc[:, bass.ds(blk, 1), :].rearrange("p b r -> p (b r)")
                dve.tensor_tensor(row, row, ps_s[:, :], ALU.add).then_inc(s_acc, 1)

            def step(i, u, prev_blk, last=False):
                g = i * SLOTS + u
                s = u % 2
                zero = isinstance(g, int) and g == 0
                early = isinstance(g, int) and g < 2
                if not last:
                    compare(g + 1, i if u + 1 < SLOTS else i + 1, (u + 1) % SLOTS)
                leaky(g, 0)
                leaky(g, 1)
                if not early:
                    dve.wait_ge(s_seg, g - 1)
                dve.tensor_tensor(leave[:, s, :, :], iota_row[:, :].unsqueeze(1).to_broadcast([P, TILES, P]),
                                  splace[:, bass.ds(g * TILES, TILES)].unsqueeze(2).to_broadcast([P, TILES, P]),
                                  ALU.is_equal).then_inc(s_leave, 1)
                leaky(g, 2)
                if not zero:
                    add_up(g - 1, prev_blk)
                dve.wait_ge(s_alphas, g + 1)
                dve.tensor_tensor(alpha[:, s, :, :], ps_g[:, :, :], alpha_s[:, :, :], ALU.max).then_inc(s_alpha, 1)
                dve.wait_ge(s_expa, g + 1)
                dve.tensor_tensor(vals[:, s, :, VALS:VALS + HEADS], expa[:, s, :, :],
                                  rows[:, u, :, D:HROW].to_broadcast([P, TILES, HEADS]),
                                  ALU.mult).then_inc(s_wgt, 1)
                dve.wait_ge(s_betas, g + 1)
                dve.tensor_tensor(beta[:, :, :], ps_b[:, :, :], beta_s[:, :, :], ALU.max).then_inc(s_beta, 1)
                dve.wait_ge(s_wgt, g + 1)
                dve.wait_ge(s_beta, g + 1)
                dve.tensor_tensor(vals[:, s, :, 0:VALS].rearrange("p t (h d) -> p t h d", d=D),
                                  beta[:, :, :].rearrange("p t (h d) -> p t h d", d=D),
                                  vals[:, s, :, VALS:VALS + HEADS].unsqueeze(3).to_broadcast([P, TILES, HEADS, D]),
                                  ALU.mult).then_inc(s_vals, 1)

            def blocks(i, shift):
                return [dve.value_load(blk_row[0:1, bass.ds(i * SLOTS + u - shift, 1)], min_val=0, max_val=BLOCKS)
                        for u in range(SLOTS)]

            compare(0, 0, 0)
            b = [dve.value_load(blk_row[0:1, u:u + 1], min_val=0, max_val=BLOCKS) for u in range(SLOTS - 1)]
            for u in range(SLOTS):
                step(0, u, b[u - 1] if u else None)
            with dve.Fori(1, BODIES - 1) as i:
                b = blocks(i, 1)
                for u in range(SLOTS):
                    step(i, u, b[u])
            b = blocks(BODIES - 1, 1) + [dve.value_load(blk_row[0:1, GROUPS - 1:GROUPS], min_val=0, max_val=BLOCKS)]
            for u in range(SLOTS):
                step(BODIES - 1, u, b[u], last=u == SLOTS - 1)
            add_up(GROUPS - 1, b[SLOTS])

            dve.wait_ge(s_acc, GROUPS)
            sums = acc[:, 0:BLOCKS, VALS:VALS + HEADS]
            link(dve.tensor_scalar(empty[:, :], acc[:, 0:BLOCKS, VROW - 1:VROW].rearrange("p b o -> p (b o)"),
                                   0.0, None, ALU.is_equal))
            link(dve.tensor_tensor(inv[:, 0, :, :], sums, empty[:, :].unsqueeze(2).to_broadcast([P, BLOCKS, HEADS]),
                                   ALU.add))
            link(dve.reciprocal(inv[:, 1, :, :], inv[:, 0, :, :]))
            link(dve.tensor_scalar(inv[:, 2, :, :], inv[:, 1, :, :], 1e-16, None, ALU.add))
            for h in range(HEADS):
                part = acc[:, 0:BLOCKS, h * D:(h + 1) * D]
                link(dve.tensor_tensor(part, part, inv[:, 2, :, h:h + 1].to_broadcast([P, BLOCKS, D]), ALU.mult))
            for h in (0, 2):
                link(dve.tensor_tensor(acc[:, 0:BLOCKS, h * D:(h + 1) * D], acc[:, 0:BLOCKS, h * D:(h + 1) * D],
                                       acc[:, 0:BLOCKS, (h + 1) * D:(h + 2) * D], ALU.add))
            link(dve.tensor_tensor(xc[:, :, :], acc[:, 0:BLOCKS, 0:D], acc[:, 0:BLOCKS, 2 * D:3 * D], ALU.add))
            dve.scalar_tensor_tensor(h32[:, :, :].rearrange("p b d -> p (b d)"), xc[:, :, :].rearrange("p b d -> p (b d)"),
                                     1.0 / HEADS, xs[:, :, :].rearrange("p b d -> p (b d)"),
                                     ALU.mult, ALU.add).then_inc(s_final, 1)

        @block.tensor
        def _(pe):
            pe.wait_ge(s_const, N_CONST)
            pe.wait_ge(s_xin, 16 * N_XIN)
            pe.transpose(ps_pos, pos_rows[:, :], ident[0:64, 0:64]).then_inc(s_wt, 1)
            pe.wait_ge(s_win, 16 * (N_WIN + HEADS))
            for c in range(PAIRS):
                for k in range(2):
                    last = pe.transpose(ps_w[c][:, k, :], w1[:, 2 * c + k, :], ident[:, :])
                last.then_inc(s_wt, 1)
            for k in range(2):
                last = pe.transpose(ps_x[:, 0, k * P:(k + 1) * P], w2[:, k, :], ident[:, :])
            last.then_inc(s_wt, 1)
            pe.wait_ge(s_count, 1)
            pe.matmul(ps_s[:, 0:BUCKETS], before[:, :], count[:, :], start=True, stop=True)
            pe.matmul(ps_s[:, BUCKETS:2 * BUCKETS], ones[:, :], count[:, :], start=True, stop=True).then_inc(s_pref, 1)
            pe.wait_ge(s_past, 1)
            pe.wait_ge(s_wcopy, 1)
            for k in range(2):
                last = pe.matmul(ps_a_flat[k][:, 0:GROUPS // 2], real[:, :],
                                 iota_group[:, k * (GROUPS // 2):(k + 1) * (GROUPS // 2)], start=True, stop=True)
            last.then_inc(s_blkp, 1)
            pe.wait_ge(s_place, 2)
            for k in range(8):
                last = pe.transpose(ps_t[:, k, :], splace_b[:, k * P:(k + 1) * P], ident_b[:, :])
            last.then_inc(s_pt, 1)
            pe.wait_ge(s_ptc, 1)
            for k in range(TC - 8):
                last = pe.transpose(ps_t[:, k, :], splace_b[:, (k + 8) * P:(k + 9) * P], ident_b[:, :])
            last.then_inc(s_pt, 1)

            def features(g, i, u):
                pe.wait_ge(s_pick, g + 1)
                pe.wait_ge(s_rows[u], (i + 1) * 32)
                if not (isinstance(g, int) and g < 1):
                    pe.wait_ge(s_feat, g)
                for part in range(2):
                    cols = slice(part * D, (part + 1) * D)
                    pe.matmul(ps_x[0:D, part, :], hblk[:, u, :].bitcast(F16)[:, cols], pick[:, u % 2, :], start=True, stop=True)
                    for t in range(TILES):
                        last = pe.matmul(ps_x[D:P, part, t * P:(t + 1) * P], rows[:, u, t, 0:D].bitcast(F16)[:, cols], ident_h[:, :],
                                         start=True, stop=True)
                last.then_inc(s_x, 1)

            def layer1(g):
                pe.wait_ge(s_feat, g + 1)
                for c in range(PAIRS):
                    if not (isinstance(g, int) and g < 1):
                        pe.wait_ge(s_hid, g * PAIRS + (c - PAIRS + 1))
                    for k in range(2):
                        o = ps_a[c][:, k, :]
                        pe.matmul(o, w1_hi[:, 2 * c + k, :], feat[:, 0, :], start=True, stop=False)
                        pe.matmul(o, w1_hi[:, 2 * c + k, :], feat[:, 1, :], start=False, stop=False)
                        last = pe.matmul(o, w1_lo[:, 2 * c + k, :], feat[:, 0, :], start=False, stop=True)
                    last.then_inc(s_l1, 1)

            def layer2(g):
                pe.wait_ge(s_hid, g * PAIRS + 1)
                if not (isinstance(g, int) and g < 1):
                    pe.wait_ge(s_alpha, g)
                for t in range(TILES):
                    for k in range(2):
                        last = pe.matmul(ps_g[:, t, :], hidden[:, 0, k, t * P:(t + 1) * P], gw2s[:, k, :],
                                         start=(k == 0), stop=(k == 1))
                last.then_inc(s_gate, 1)
                if not (isinstance(g, int) and g < 1):
                    pe.wait_ge(s_beta, g)
                for h in range(HEADS):
                    if h % 2 == 0:
                        pe.wait_ge(s_hid, g * PAIRS + (h // 2 + 2))
                    for t in range(TILES):
                        last = pe.matmul(ps_b[:, t, h * D:(h + 1) * D],
                                         hidden[:, 1 + h // 2, h % 2, t * P:(t + 1) * P], w2t[:, h, :],
                                         start=True, stop=True)
                last.then_inc(s_l2, 1)

            def segment(g, s):
                pe.wait_ge(s_leave, g + 1)
                pe.wait_ge(s_vals, g + 1)
                if not (isinstance(g, int) and g < 1):
                    pe.wait_ge(s_acc, g)
                for t in range(TILES):
                    last = pe.matmul(ps_s[:, :], leave[:, s, t, :], vals[:, s, t, :],
                                     start=(t == 0), stop=(t == TILES - 1))
                last.then_inc(s_seg, 1)

            def step(i, u, last=False):
                g = i * SLOTS + u
                layer1(g)
                if not (isinstance(g, int) and g < 1):
                    segment(g - 1, (u - 1) % 2)
                if not last:
                    features(g + 1, i if u + 1 < SLOTS else i + 1, (u + 1) % SLOTS)
                layer2(g)

            pe.wait_ge(s_wcopy, 1)
            features(0, 0, 0)
            for u in range(SLOTS):
                step(0, u)
            with pe.Fori(1, BODIES - 1) as i:
                for u in range(SLOTS):
                    step(i, u)
            for u in range(SLOTS):
                step(BODIES - 1, u, last=u == SLOTS - 1)
            segment(GROUPS - 1, (SLOTS - 1) % 2)


_INS = ['x', 'src', 'dst', 'node_vec', 'L0_gnn_gate_w1', 'L0_gnn_gate_w2', 'L0_gnn_msg_w1', 'L0_gnn_msg_w2']
_OUTS = [((6250, 64), 'float32')]


def kernel(**inputs):
    import numpy as _np
    import concourse.bacc as _bacc
    from concourse import mybir as _mybir
    from concourse.bass_utils import run_bass_kernel_spmd as _run

    nc = _bacc.Bacc("TRN2", target_bir_lowering=False, num_devices=1)
    arrays, args = {}, []
    for name in _INS:
        a = _np.ascontiguousarray(inputs[name])
        arrays[f"in_{name}_dram"] = a
        args.append(nc.dram_tensor(f"in_{name}_dram", a.shape, _mybir.dt.from_np(a.dtype), kind="ExternalInput").ap())
    for i, (shape, dtype) in enumerate(_OUTS):
        dt = _mybir.dt.from_np(_np.dtype(dtype))
        args.append(nc.dram_tensor(f"out_{i}_dram", shape, dt, kind="ExternalOutput").ap())
    gnn_preln_kernel(nc, *args)
    r = _run(nc, [arrays], core_ids=[0])
    got = tuple(r.results[0][f"out_{i}_dram"] for i in range(len(_OUTS)))
    return got[0]
```

```python
from contextlib import ExitStack

import concourse.bass as bass
from concourse import mybir

F32 = mybir.dt.float32
F16 = mybir.dt.float16
BF16 = mybir.dt.bfloat16
I32 = mybir.dt.int32
ALU = mybir.AluOpType
ACT = mybir.ActivationFunctionType
AX = mybir.AxisListType
RMAX = bass.bass_isa.ReduceOp.max

P = 128
NEG_SLOPE = 0.2
EPS = 1e-5
GROUP = 256
TILES = GROUP // P
SLOTS = 6
BATCH = 8
H_SCALE = 256.0
PAD_KEY = 255


def gnn_preln_kernel(nc, x, src, dst, node_vec, gate_w1, gate_w2, msg_w1, msg_w2, out):
    N, D = x.shape
    E = src.shape[0]
    HEADS, G_HID, _ = msg_w1.shape
    F_HID = gate_w1.shape[1]
    assert D == 64 and G_HID == P and F_HID == 64 and HEADS == 4

    BLOCKS = -(-N // P)
    LAST = N - (BLOCKS - 1) * P
    BUCKETS = BLOCKS + 1
    NJ = -(-E // P)
    NJ += -NJ % (2 * BATCH)
    FULL = E // NJ
    REST = E - FULL * NJ
    GROUPS = (P * NJ + BUCKETS * (GROUP - 1)) // GROUP
    GROUPS += -GROUPS % SLOTS
    BODIES = GROUPS // SLOTS
    T = GROUPS * TILES
    TC = -(-T // P)
    HID_CHUNKS = (HEADS * F_HID + HEADS * G_HID) // P
    PAIRS = HID_CHUNKS // 2
    VALS = HEADS * D
    VROW = VALS + HEADS + 1
    HROW = D + 1
    assert FULL == P - 1 and BUCKETS <= F_HID and D * 2 == P

    key_d = nc.dram_tensor("key_d", [P, T], I32).ap()
    key_flat = key_d.rearrange("p (t o) -> (p t) o", o=1)
    place_d = nc.dram_tensor("place_d", [TC * P, P], BF16).ap()
    place_flat = place_d.rearrange("t p -> (t p)")
    node_d = nc.dram_tensor("node_d", [BUCKETS * P, HROW], F32).ap()

    with ExitStack() as ctx:
        def sb(name, shape, dt):
            return ctx.enter_context(nc.sbuf_tensor(name, shape, dt))

        def ps(name, shape, dt=F32):
            return ctx.enter_context(nc.psum_tensor(name, shape, dt))

        def sem(name):
            return ctx.enter_context(nc.semaphore(name))

        ident = sb("ident", [P, P], F32)
        ident_h = sb("ident_h", [P, P], F16)
        ident_b = sb("ident_b", [P, P], BF16)
        before = sb("before", [P, P], F32)
        real = sb("real", [P, P], F32)
        ones = sb("ones", [P, P], F32)
        iota_row = sb("iota_row", [P, P], F32)
        iota_col = sb("iota_col", [P, 1], F32)
        iota_group = sb("iota_group", [P, GROUPS], F32)
        xs = sb("xs", [P, BLOCKS, D], F32)
        xc = sb("xc", [P, BLOCKS, D], F32)
        node = sb("node", [P, BUCKETS, HROW], F32)
        node_h = node[:, 0:BLOCKS, 0:D].bitcast(F16)
        stat = sb("stat", [P, 6, BLOCKS], F32)
        pos_rows = sb("pos_rows", [64, P], F32)
        w1 = sb("w1", [P, HID_CHUNKS, P], F32)
        w1_hi = sb("w1_hi", [P, HID_CHUNKS, P], F16)
        w1_lo = sb("w1_lo", [P, HID_CHUNKS, P], F16)
        w2 = sb("w2", [P, 2, P], F32)
        w2t = sb("w2t", [P, HEADS, D], F32)
        gw2 = sb("gw2", [P, 2, HEADS], F32)
        gw2s = sb("gw2s", [P, 2, HEADS], F32)
        wmax = sb("wmax", [P, 6], F32)
        wexp = sb("wexp", [P, 3], I32)
        acc = sb("acc", [P, BUCKETS, VROW], F32)
        work = acc[:, :, :].rearrange("p b r -> p (b r)")[:, 0:8 * NJ].rearrange("p (k j) -> p k j", j=NJ)
        h32 = work[:, 6:8, :].rearrange("p k j -> p (k j)")[:, 0:BLOCKS * D].rearrange("p (b d) -> p b d", d=D)
        src_i, blk_i, rank_p, rank_t = (work[:, k, :].bitcast(I32) for k in range(4))
        cum, rank, picked = work[:, 4, :], work[:, 5, :], work[:, 6:8, :]
        dst_i = sb("dst_i", [P, NJ], I32)
        blk_b = sb("blk_b", [P, NJ], BF16)
        ones_b = sb("ones_b", [P, NJ], BF16)
        sign_out = sb("sign_out", [P, NJ], BF16)
        bias = sb("bias", [P, 1], F32)
        sign_sum = sb("sign_sum", [P, BUCKETS + 1], F32)
        count = sb("count", [P, BUCKETS], F32)
        tot = sb("tot", [P, BUCKETS], F32)
        grp_i = sb("grp_i", [P, BUCKETS], I32)
        grp = sb("grp", [P, BUCKETS], F32)
        cum_grp = sb("cum_grp", [P, BUCKETS], F32)
        start = sb("start", [P, BUCKETS], F32)
        end_col = sb("end_col", [P, 1], F32)
        tmp_b = sb("tmp_b", [P, BUCKETS], F32)
        blk_row = sb("blk_row", [P, GROUPS], I32)
        bucket = sb("bucket", [P, 1], F32)
        first = sb("first", [P, 1], F32)
        mask = sb("mask", [P, NJ], BF16)
        rank_i = sb("rank_i", [P, NJ], I32)
        stage_key = sb("stage_key", [P, 2, BATCH], I32)
        stage_addr = sb("stage_addr", [P, 2, BATCH], I32)
        skey = sb("skey", [P, T], I32)
        sdst = sb("sdst", [P, T], I32)
        splace = sb("splace", [P, T], F32)
        splace_b = sb("splace_b", [P, TC * P], BF16)
        place_t = sb("place_t", [P, TC, P], BF16)
        idx = sb("idx", [P, SLOTS, TILES], I32)
        rows = sb("rows", [P, SLOTS, TILES, HROW], F32)
        place_bc = sb("place_bc", [P, SLOTS, GROUP], BF16)
        hblk = sb("hblk", [P, SLOTS, D], F32)
        pick = sb("pick", [P, 2, GROUP], F16)
        feat = sb("feat", [P, 2, 2, GROUP], F16)
        hidden = sb("hidden", [P, 2, PAIRS, 2, GROUP], F32)
        alpha = sb("alpha", [P, 2, TILES, HEADS], F32)
        expa = sb("expa", [P, 2, TILES, HEADS], F32)
        hid_s = sb("hid_s", [P, PAIRS, 2, GROUP], F32)
        alpha_s = sb("alpha_s", [P, TILES, HEADS], F32)
        beta_s = sb("beta_s", [P, TILES, VALS], F32)
        beta = sb("beta", [P, 2, TILES, VALS], F32)
        vals = sb("vals", [P, 2, TILES, VROW], F32)
        leave = sb("leave", [P, 2, TILES, P], F32)
        inv = sb("inv", [P, 3, BLOCKS, HEADS], F32)
        empty = sb("empty", [P, BLOCKS], F32)

        ps_a = [ps(f"ps_a{c}", [P, 2, GROUP]) for c in range(PAIRS)]
        ps_x = ps("ps_x", [P, 2, GROUP])
        ps_b = ps("ps_b", [P, TILES, VALS])
        ps_g = ps("ps_g", [P, 512])[:, 0:TILES * HEADS].rearrange("p (t h) -> p t h", h=HEADS)
        ps_s = ps("ps_s", [P, 512])[:, 0:VROW]
        ps_t = ps("ps_t", [P, 8, P], BF16)

        ps_pos = ps_b[:, :, :].rearrange("p t v -> p (t v)")[:, 0:64]
        ps_a_flat = [ps_a[c][:, :, :].rearrange("p a g -> p (a g)") for c in range(PAIRS)]
        ps_w = [ps_a[c][:, 0, :].rearrange("p (a e) -> p a e", a=2) for c in range(PAIRS)]

        s_const = sem("s_const")
        s_pre = sem("s_pre")
        s_xin = sem("s_xin")
        s_win = sem("s_win")
        s_ein = sem("s_ein")
        s_pad = sem("s_pad")
        s_v = sem("s_v")
        s_var = sem("s_var")
        s_std = sem("s_std")
        s_wt = sem("s_wt")
        s_wmax = sem("s_wmax")
        s_wmaxa = sem("s_wmaxa")
        s_wcopy = sem("s_wcopy")
        s_node = sem("s_node")
        s_nout = sem("s_nout")
        s_blk = sem("s_blk")
        s_bias = sem("s_bias")
        s_sign = sem("s_sign")
        s_count = sem("s_count")
        s_pref = sem("s_pref")
        s_past = sem("s_past")
        s_blkp = sem("s_blkp")
        s_blkrow = sem("s_blkrow")
        s_first = sem("s_first")
        s_mask = sem("s_mask")
        s_cum = sem("s_cum")
        s_picked = sem("s_picked")
        s_rank = sem("s_rank")
        s_addr = sem("s_addr")
        s_staged = sem("s_staged")
        s_seen = sem("s_seen")
        s_scat = [sem(f"s_scat{u}") for u in range(2)]
        s_skey = sem("s_skey")
        s_place = sem("s_place")
        s_pt = sem("s_pt")
        s_ptc = sem("s_ptc")
        s_pout = sem("s_pout")
        s_idx = sem("s_idx")
        s_rows = [sem(f"s_rows{u}") for u in range(SLOTS)]
        s_in = [sem(f"s_in{u}") for u in range(SLOTS)]
        s_pick = sem("s_pick")
        s_x = sem("s_x")
        s_feat = sem("s_feat")
        s_l1 = sem("s_l1")
        s_hid = sem("s_hid")
        s_gate = sem("s_gate")
        s_hids = sem("s_hids")
        s_alphas = sem("s_alphas")
        s_betas = sem("s_betas")
        s_alpha = sem("s_alpha")
        s_expa = sem("s_expa")
        s_l2 = sem("s_l2")
        s_beta = sem("s_beta")
        s_wgt = sem("s_wgt")
        s_vals = sem("s_vals")
        s_leave = sem("s_leave")
        s_seg = sem("s_seg")
        s_acc = sem("s_acc")
        s_clear = sem("s_clear")
        s_final = sem("s_final")
        s_out = sem("s_out")

        block = ctx.enter_context(nc.Block())

        N_CONST = 11
        N_XIN = 4
        N_WIN = 6

        @block.sync
        def _(sp):
            sp.wait_ge(s_pre, 5)
            sp.dma_start(src_i[0:FULL, :], src[0:FULL * NJ].rearrange("(p j) -> p j", j=NJ)).then_inc(s_ein, 16)
            sp.dma_start(src_i[FULL:FULL + 1, 0:REST], src[FULL * NJ:E].rearrange("(p j) -> p j", p=1)).then_inc(s_ein, 16)
            sp.dma_start(dst_i[0:FULL, :], dst[0:FULL * NJ].rearrange("(p j) -> p j", j=NJ)).then_inc(s_ein, 16)
            sp.dma_start(dst_i[FULL:FULL + 1, 0:REST], dst[FULL * NJ:E].rearrange("(p j) -> p j", p=1)).then_inc(s_ein, 16)
            sp.dma_start(xs[:, 0:BLOCKS - 1, :],
                         x[0:(BLOCKS - 1) * P, :].rearrange("(b p) d -> p b d", p=P)).then_inc(s_xin, 16)
            sp.dma_start(xs[0:LAST, BLOCKS - 1, :], x[(BLOCKS - 1) * P:N, :]).then_inc(s_xin, 16)
            sp.dma_start(pos_rows[0:BLOCKS - 1, :],
                         node_vec[0:(BLOCKS - 1) * P].rearrange("(b p) -> b p", p=P)).then_inc(s_xin, 16)
            sp.dma_start(pos_rows[BLOCKS - 1:BLOCKS, 0:LAST],
                         node_vec[(BLOCKS - 1) * P:N].rearrange("(b p) -> b p", b=1)).then_inc(s_xin, 16)
            sp.dma_start(w1[:, 0:2, :], gate_w1.rearrange("(c a) f e -> (a f) c e", a=2)).then_inc(s_win, 16)
            sp.dma_start(w1[:, 2:2 + HEADS, :], msg_w1.rearrange("h f e -> f h e")).then_inc(s_win, 16)
            for h in range(HEADS):
                sp.dma_start(w2[(h % 2) * D:(h % 2 + 1) * D, h // 2, :], msg_w2[h, :, :]).then_inc(s_win, 16)
            sp.dma_start(key_d, skey[:, :]).then_inc(s_pad, 16)
            sp.wait_ge(s_node, 1)
            sp.dma_start(node_d.rearrange("(b p) r -> p b r", p=P), node[:, :, :]).then_inc(s_nout, 16)
            for u in range(2):
                sp.wait_ge(s_scat[u], 16 * NJ // 2)
            sp.dma_start(skey[:, :], key_d).then_inc(s_skey, 16)
            sp.wait_ge(s_ptc, 2)
            sp.dma_start(place_d.rearrange("(a t) p -> t a p", t=P), place_t[:, :, :]).then_inc(s_pout, 16)
            sp.wait_ge(s_pout, 16)
            sp.wait_ge(s_nout, 16)
            sp.wait_ge(s_blkrow, 1)

            def load(g, i, u):
                blk = sp.value_load(blk_row[0:1, bass.ds(g, 1)], min_val=0, max_val=BLOCKS)
                if i is not None:
                    sp.wait_ge(s_x, SLOTS * i + u - SLOTS + 1)
                    sp.wait_ge(s_pick, SLOTS * i + u - SLOTS + 1)
                sp.dma_start(hblk[:, u, :], node_d[bass.ds(blk * P, P), 0:D]).then_inc(s_in[u], 16)
                sp.dma_start(place_bc[:, u, :],
                             place_flat[bass.ds(g * GROUP, GROUP)].rearrange("(o n) -> o n", o=1)
                             .to_broadcast([P, GROUP])).then_inc(s_in[u], 16)

            for u in range(SLOTS):
                load(u, None, u)
            with sp.Fori(1, BODIES) as i:
                for u in range(SLOTS):
                    load(i * SLOTS + u, i, u)
            sp.wait_ge(s_final, 1)
            sp.dma_start(out[0:(BLOCKS - 1) * P, :].rearrange("(b p) d -> p b d", p=P),
                         xc[:, 0:BLOCKS - 1, :]).then_inc(s_out, 16)
            sp.dma_start(out[(BLOCKS - 1) * P:N, :], xc[0:LAST, BLOCKS - 1, :]).then_inc(s_out, 16)
            sp.wait_ge(s_out, 32)

        @block.gpsimd
        def _(pool):
            pool.memset(ident[:, :], 0.0).then_inc(s_const, 1)
            pool.memset(ones[:, :], 1.0).then_inc(s_const, 1)
            pool.iota(iota_row[:, :], pattern=[[1, P]], base=0, channel_multiplier=0,
                      allow_small_or_imprecise_dtypes=True).then_inc(s_const, 1)
            pool.iota(iota_col[:, :], pattern=[[1, 1]], base=0, channel_multiplier=1,
                      allow_small_or_imprecise_dtypes=True).then_inc(s_const, 1)
            pool.iota(iota_group[:, :], pattern=[[1, GROUPS]], base=0, channel_multiplier=0,
                      allow_small_or_imprecise_dtypes=True).then_inc(s_const, 1)
            pool.wait_ge(s_const, 5)
            pool.affine_select(out=ident[:, :], in_=ident[:, :], compare_op=ALU.not_equal, fill=1.0,
                               base=0, pattern=[[-1, P]], channel_multiplier=1).then_inc(s_const, 1)
            pool.affine_select(out=before[:, :], in_=ones[:, :], compare_op=ALU.is_gt, fill=0.0,
                               base=0, pattern=[[1, P]], channel_multiplier=-1).then_inc(s_const, 1)
            pool.affine_select(out=real[:, :], in_=ones[:, :], compare_op=ALU.is_gt, fill=0.0,
                               base=BLOCKS, pattern=[[0, P]], channel_multiplier=-1).then_inc(s_const, 1)
            pool.wait_ge(s_const, 8)
            pool.tensor_copy(ident_h[:, :], ident[:, :]).then_inc(s_const, 1)
            pool.tensor_copy(ident_b[:, :], ident[:, :]).then_inc(s_const, 1)
            pool.memset(rank[:, :], 0.0).then_inc(s_const, 1)
            pool.wait_ge(s_wmax, 1)
            pool.partition_all_reduce(wmax[:, 1:2], wmax[:, 0:1], P, RMAX).then_inc(s_wmaxa, 1)
            pool.wait_ge(s_const, N_CONST)
            pool.wait_ge(s_picked, 1)
            pool.tensor_tensor(rank[:, :], rank[:, :], picked[:, 0, :], ALU.add).then_inc(s_rank, 1)
            pool.wait_ge(s_picked, 2)
            pool.wait_ge(s_rank, 1)
            pool.tensor_tensor(rank[:, :], rank[:, :], picked[:, 1, :], ALU.add).then_inc(s_rank, 1)
            with pool.Fori(1, BUCKETS // 2) as b2:
                for u in range(2):
                    pool.wait_ge(s_picked, b2 * 2 + u + 1)
                    pool.wait_ge(s_rank, b2 * 2 + u)
                    pool.tensor_tensor(rank[:, :], rank[:, :], picked[:, u, :], ALU.add).then_inc(s_rank, 1)

            pool.wait_ge(s_pad, 16)

            def scatter(staged, u):
                pool.wait_ge(s_staged, staged)
                pool.sem_inc(s_seen, 1)
                for k in range(BATCH):
                    pool.indirect_dma_start(
                        out=key_flat, out_offset=bass.IndirectOffsetOnAxis(ap=stage_addr[:, u, k:k + 1], axis=0),
                        in_=stage_key[:, u, k:k + 1], in_offset=None).then_inc(s_scat[u], 16)

            with pool.Fori(0, NJ // (2 * BATCH)) as j:
                for u in range(2):
                    scatter(j * 4 + (2 * u + 2), u)

            pool.wait_ge(s_place, 1)
            pool.wait_ge(s_nout, 16)

            def gather(g, i, u):
                if i is not None:
                    pool.wait_ge(s_rows[u], i * 32)
                    pool.wait_ge(s_x, g - (SLOTS - 1))
                    pool.wait_ge(s_wgt, g - (SLOTS - 1))
                    pool.sem_inc(s_seen, 1)
                pool.tensor_copy(idx[:, u, :], sdst[:, bass.ds(g * TILES, TILES)]).then_inc(s_idx, 1)
                pool.wait_ge(s_idx, g + 1)
                pool.sem_inc(s_seen, 1)
                for t in range(TILES):
                    pool.indirect_dma_start(
                        out=rows[:, u, t, :], out_offset=None, in_=node_d,
                        in_offset=bass.IndirectOffsetOnAxis(ap=idx[:, u, t:t + 1], axis=0)).then_inc(s_rows[u], 16)

            def weigh(g, s):
                pool.wait_ge(s_wgt, g + 1)
                pool.wait_ge(s_beta, g + 1)
                pool.tensor_tensor(vals[:, s, :, 0:VALS].rearrange("p t (h d) -> p t h d", d=D),
                                   beta[:, s, :, :].rearrange("p t (h d) -> p t h d", d=D),
                                   vals[:, s, :, VALS:VALS + HEADS].unsqueeze(3).to_broadcast([P, TILES, HEADS, D]),
                                   ALU.mult).then_inc(s_vals, 1)

            def step(i, u, last=False):
                g = i * SLOTS + u
                if u == 0:
                    if not (isinstance(i, int) and i == 0):
                        gather(g + SLOTS - 1, i, SLOTS - 1)
                elif not last:
                    gather(g + SLOTS - 1, i + 1, u - 1)
                weigh(g, u % 2)

            for u in range(SLOTS):
                gather(u, None, u)
            for u in range(SLOTS):
                step(0, u)
            with pool.Fori(1, BODIES - 1) as i:
                for u in range(SLOTS):
                    step(i, u)
            for u in range(SLOTS):
                step(BODIES - 1, u, last=True)

        @block.scalar
        def _(act):
            act.wait_ge(s_pre, 5)
            for h in range(HEADS):
                act.dma_start(gw2[(h % 2) * F_HID:(h % 2 + 1) * F_HID, h // 2, h:h + 1],
                              gate_w2[h, :, :].rearrange("o f -> f o")).then_inc(s_win, 16)
            act.wait_ge(s_var, 1)
            act.activation(stat[:, 3, :], stat[:, 2, :], ACT.Sqrt).then_inc(s_std, 1)
            act.wait_ge(s_blk, 1)
            act.activation(sign_out[:, :], blk_b[:, :], ACT.Sign, bias=bias[:, 0:1],
                           accum_out=sign_sum[:, 0:1]).then_inc(s_sign, 1)
            with act.Fori(1, BUCKETS) as b:
                act.wait_ge(s_sign, b)
                act.activation(bias[:, :], bias[:, :], ACT.Copy, bias=-1.0).then_inc(s_bias, 1)
                act.wait_ge(s_bias, b)
                act.activation(sign_out[:, :], blk_b[:, :], ACT.Sign, bias=bias[:, 0:1],
                               accum_out=sign_sum[:, bass.ds(b, 1)]).then_inc(s_sign, 1)

            def scaled(g, c):
                act.wait_ge(s_l1, g * PAIRS + c + 1)
                if not (isinstance(g, int) and g < 1):
                    act.wait_ge(s_hid, g * PAIRS + (c - PAIRS + 1))
                act.activation(hid_s[:, c, :, :], ps_a[c][:, :, :], ACT.Copy, scale=NEG_SLOPE).then_inc(s_hids, 1)

            def copy_feat(g, s):
                act.wait_ge(s_x, g + 1)
                act.activation(feat[:, s, :, :], ps_x[:, :, :], ACT.Copy).then_inc(s_feat, 1)

            def step(g, s, left=3):
                early = isinstance(g, int) and g < 2
                if left > 2:
                    copy_feat(g + 2, s)
                if left > 1:
                    for c in range(PAIRS):
                        scaled(g + 1, c)
                act.wait_ge(s_gate, g + 1)
                if not (isinstance(g, int) and g < 1):
                    act.wait_ge(s_alpha, g)
                act.activation(alpha_s[:, :, :], ps_g[:, :, :], ACT.Copy, scale=NEG_SLOPE).then_inc(s_alphas, 1)
                act.wait_ge(s_alpha, g + 1)
                if not early:
                    act.wait_ge(s_wgt, g - 1)
                act.activation(expa[:, s, :, :], alpha[:, s, :, :], ACT.Exp).then_inc(s_expa, 1)
                act.wait_ge(s_l2, g + 1)
                if not (isinstance(g, int) and g < 1):
                    act.wait_ge(s_beta, g)
                act.activation(beta_s[:, :, :], ps_b[:, :, :], ACT.Copy, scale=NEG_SLOPE).then_inc(s_betas, 1)

            copy_feat(0, 0)
            copy_feat(1, 1)
            for c in range(PAIRS):
                scaled(0, c)
            for u in range(SLOTS):
                step(u, u % 2)
            with act.Fori(1, BODIES - 1) as i:
                for u in range(SLOTS):
                    step(i * SLOTS + u, u % 2)
            for u in range(SLOTS):
                step((BODIES - 1) * SLOTS + u, u % 2, left=SLOTS - u)

        @block.vector
        def _(dve):
            chain = [0]

            def link(ins):
                chain[0] += 1
                ins.then_inc(s_v, 1)
                dve.wait_ge(s_v, chain[0])

            dve.memset(src_i[96:P, :], BLOCKS * P).then_inc(s_pre, 1)
            dve.memset(dst_i[96:P, :], 0).then_inc(s_pre, 1)
            dve.memset(xs[:, BLOCKS - 1, :], 0.0).then_inc(s_pre, 1)
            dve.memset(gw2[:, :, :], 0.0)
            dve.memset(pos_rows[:, :], 0.0).then_inc(s_pre, 1)
            dve.memset(skey[:, :], PAD_KEY).then_inc(s_pre, 1)
            dve.memset(ones_b[:, :], 1.0)
            dve.memset(vals[:, :, :, VROW - 1:VROW], 1.0)
            dve.memset(splace_b[:, T:TC * P], float(PAD_KEY))
            link(dve.memset(node[:, :, :], 0.0))

            dve.memset(bias[:, :], 0.5)
            dve.memset(bucket[:, :], 0.0)
            dve.wait_ge(s_ein, 64)
            link(dve.tensor_scalar(blk_i[:, :], src_i[:, :], 7, None, ALU.logical_shift_right))
            dve.tensor_copy(blk_b[:, :], blk_i[:, :]).then_inc(s_blk, 1)
            link(dve.tensor_scalar(rank_i[:, :], src_i[:, :], P - 1, None, ALU.bitwise_and))
            link(dve.scalar_tensor_tensor(dst_i[:, :], dst_i[:, :], 256.0, rank_i[:, :], ALU.mult, ALU.add))

            dve.wait_ge(s_xin, 16 * N_XIN)
            link(dve.tensor_reduce(stat[:, 0, :], xs[:, :, :], AX.X, ALU.add))
            link(dve.tensor_scalar(stat[:, 1, :], stat[:, 0, :], 1.0 / D, None, ALU.mult))
            link(dve.tensor_tensor(xc[:, :, :], xs[:, :, :],
                                   stat[:, 1, :].unsqueeze(2).to_broadcast([P, BLOCKS, D]), ALU.subtract))
            link(dve.tensor_tensor(h32[:, :, :], xc[:, :, :], xc[:, :, :], ALU.mult))
            link(dve.tensor_reduce(stat[:, 0, :], h32[:, :, :], AX.X, ALU.add))
            dve.tensor_scalar(stat[:, 2, :], stat[:, 0, :], 1.0 / D, EPS, ALU.mult, ALU.add).then_inc(s_var, 1)
            dve.wait_ge(s_std, 1)
            link(dve.reciprocal(stat[:, 4, :], stat[:, 3, :]))
            link(dve.tensor_scalar(stat[:, 5, :], stat[:, 4, :], H_SCALE, None, ALU.mult))
            link(dve.tensor_tensor(xc[:, :, :], xc[:, :, :],
                                   stat[:, 5, :].unsqueeze(2).to_broadcast([P, BLOCKS, D]), ALU.mult))
            link(dve.tensor_scalar(h32[:, :, :], xc[:, :, :], 0.0, None, ALU.max))
            link(dve.tensor_copy(node_h[:, :, 0:D], h32[:, :, :]))
            link(dve.tensor_tensor(node_h[:, :, D:2 * D], h32[:, :, :], node_h[:, :, 0:D], ALU.subtract))
            dve.wait_ge(s_wt, 1)
            dve.tensor_copy(node[:, 0:BLOCKS, D:HROW].rearrange("p b o -> p (b o)"),
                            ps_pos[:, 0:BLOCKS]).then_inc(s_node, 1)

            dve.wait_ge(s_win, 16 * (N_WIN + HEADS))
            link(dve.tensor_reduce(wmax[:, 2:3], w1[:, :, :].rearrange("p c e -> p (c e)"), AX.X, ALU.max))
            link(dve.tensor_reduce(wmax[:, 3:4], w1[:, :, :].rearrange("p c e -> p (c e)"), AX.X, ALU.min))
            link(dve.tensor_scalar(wmax[:, 4:5], wmax[:, 3:4], -1.0, 1e-30, ALU.mult, ALU.max))
            dve.tensor_tensor(wmax[:, 0:1], wmax[:, 2:3], wmax[:, 4:5], ALU.max).then_inc(s_wmax, 1)
            dve.wait_ge(s_wmaxa, 1)
            link(dve.tensor_scalar(wexp[:, 0:1], wmax[:, 1:2].bitcast(I32), 23, None, ALU.logical_shift_right))
            link(dve.tensor_scalar(wexp[:, 1:2], wexp[:, 0:1], -1.0, 264.0, ALU.mult, ALU.add))
            link(dve.tensor_scalar(wexp[:, 2:3], wexp[:, 0:1], -10.0, None, ALU.add))
            link(dve.tensor_scalar(wexp[:, 1:3], wexp[:, 1:3], 23, None, ALU.logical_shift_left))
            scale = wexp[:, 1:2].bitcast(F32)
            unscale = wexp[:, 2:3].bitcast(F32)
            dve.wait_ge(s_wt, 1 + PAIRS)
            for c in range(PAIRS):
                link(dve.tensor_scalar(w1[:, 2 * c:2 * c + 2, :], ps_w[c], scale, None, ALU.mult))
            link(dve.tensor_copy(w1_hi[:, :, :], w1[:, :, :]))
            link(dve.tensor_tensor(w1_lo[:, :, :], w1[:, :, :], w1_hi[:, :, :], ALU.subtract))
            dve.wait_ge(s_wt, 5)
            link(dve.tensor_scalar(w2t[:, :, :], ps_x[:, 0, :].rearrange("p (h d) -> p h d", d=D),
                                   unscale, 1.0 / H_SCALE, ALU.mult, ALU.mult))
            dve.tensor_scalar(gw2s[:, :, :], gw2[:, :, :], unscale, 1.0 / H_SCALE,
                              ALU.mult, ALU.mult).then_inc(s_wcopy, 1)

            dve.wait_ge(s_sign, BUCKETS)
            link(dve.memset(sign_sum[:, BUCKETS:BUCKETS + 1], -float(NJ)))
            link(dve.tensor_tensor(count[:, :], sign_sum[:, 0:BUCKETS], sign_sum[:, 1:BUCKETS + 1], ALU.subtract))
            dve.tensor_scalar(count[:, :], count[:, :], 0.5, None, ALU.mult).then_inc(s_count, 1)
            dve.wait_ge(s_pref, 1)
            link(dve.tensor_scalar(grp_i[:, :], ps_s[:, BUCKETS:2 * BUCKETS], float(GROUP - 1), None, ALU.add))
            link(dve.tensor_scalar(grp_i[:, :], grp_i[:, :], GROUP.bit_length() - 1, None, ALU.logical_shift_right))
            link(dve.tensor_copy(grp[:, :], grp_i[:, :]))
            link(dve.tensor_tensor_scan(cum_grp[:, :], ones[:, 0:BUCKETS], grp[:, :], 0.0, ALU.mult, ALU.add))
            link(dve.tensor_tensor(tmp_b[:, :], cum_grp[:, :], grp[:, :], ALU.subtract))
            link(dve.scalar_tensor_tensor(start[:, :], tmp_b[:, :], float(GROUP), ps_s[:, 0:BUCKETS], ALU.mult, ALU.add))
            link(dve.tensor_scalar(start[:, :], start[:, :], -1.0, None, ALU.add))
            link(dve.tensor_tensor(tmp_b[:, :], cum_grp[:, :], ident[:, 0:BUCKETS], ALU.mult))
            link(dve.tensor_reduce(end_col[:, :], tmp_b[:, :], AX.X, ALU.add))
            dve.tensor_scalar(iota_group[:, :], iota_group[:, :], end_col[:, 0:1], None, ALU.is_ge).then_inc(s_past, 1)
            dve.wait_ge(s_blkp, 1)
            dve.tensor_copy(blk_row[:, 0:GROUPS // 2], ps_a_flat[0][:, 0:GROUPS // 2])
            dve.tensor_copy(blk_row[:, GROUPS // 2:GROUPS], ps_a_flat[1][:, 0:GROUPS // 2]).then_inc(s_blkrow, 1)

            def bucket_places(b, u):
                dve.tensor_copy(first[:, :], start[:, bass.ds(b, 1)]).then_inc(s_first, 1)
                dve.tensor_scalar(mask[:, :], blk_b[:, :], bucket[:, 0:1], None, ALU.is_equal).then_inc(s_mask, 1)
                dve.wait_ge(s_mask, b + 1)
                dve.wait_ge(s_first, 2 * b + 1)
                dve.tensor_tensor_scan(cum[:, :], ones_b[:, :], mask[:, :], first[:, 0:1],
                                       ALU.mult, ALU.add).then_inc(s_cum, 1)
                dve.tensor_scalar(bucket[:, :], bucket[:, :], 1.0, None, ALU.add).then_inc(s_first, 1)
                dve.wait_ge(s_cum, b + 1)
                if not isinstance(b, int):
                    dve.wait_ge(s_rank, b - 1)
                dve.tensor_tensor(picked[:, u, :], cum[:, :], mask[:, :], ALU.mult).then_inc(s_picked, 1)
                dve.wait_ge(s_picked, b + 1)
                dve.wait_ge(s_first, 2 * b + 2)

            for u in range(2):
                bucket_places(u, u)
            with dve.Fori(1, BUCKETS // 2) as b2:
                for u in range(2):
                    bucket_places(b2 * 2 + u, u)

            dve.wait_ge(s_rank, BUCKETS)
            link(dve.tensor_copy(rank_i[:, :], rank[:, :]))
            dve.tensor_scalar(rank_p[:, :], rank_i[:, :], P - 1, None, ALU.bitwise_and)
            link(dve.tensor_scalar(rank_t[:, :], rank_i[:, :], 7, None, ALU.logical_shift_right))
            link(dve.scalar_tensor_tensor(rank_i[:, :], rank_p[:, :], float(T), rank_t[:, :], ALU.mult, ALU.add))

            dve.memset(acc[:, :, :], 0.0).then_inc(s_clear, 1)

            def stage(j, u):
                dve.tensor_copy(stage_addr[:, u, :], rank_i[:, bass.ds(j, BATCH)]).then_inc(s_staged, 1)
                dve.tensor_copy(stage_key[:, u, :], dst_i[:, bass.ds(j, BATCH)]).then_inc(s_staged, 1)

            for u in range(2):
                stage(u * BATCH, u)
            with dve.Fori(1, NJ // (2 * BATCH)) as j:
                for u in range(2):
                    dve.wait_ge(s_scat[u], j * (16 * BATCH))
                    stage(j * (2 * BATCH) + u * BATCH, u)

            dve.wait_ge(s_skey, 16)
            dve.tensor_scalar(sdst[:, :], skey[:, :], 8, None, ALU.logical_shift_right).then_inc(s_place, 1)
            link(dve.tensor_scalar(skey[:, :], skey[:, :], 255, None, ALU.bitwise_and))
            dve.tensor_copy(splace[:, :], skey[:, :])
            dve.tensor_copy(splace_b[:, 0:T], skey[:, :]).then_inc(s_place, 1)
            dve.wait_ge(s_pt, 1)
            dve.tensor_copy(place_t[:, 0:8, :], ps_t[:, :, :]).then_inc(s_ptc, 1)
            dve.wait_ge(s_pt, 2)
            dve.tensor_copy(place_t[:, 8:TC, :], ps_t[:, 0:TC - 8, :]).then_inc(s_ptc, 1)

            def compare(g, i, u):
                dve.wait_ge(s_in[u], (i + 1) * 32)
                if not (isinstance(g, int) and g < 2):
                    dve.wait_ge(s_x, g - 1)
                dve.tensor_scalar(pick[:, u % 2, :], place_bc[:, u, :], iota_col[:, 0:1], None,
                                  ALU.is_equal).then_inc(s_pick, 1)

            def leaky(g, s, c):
                dve.wait_ge(s_hids, g * PAIRS + c + 1)
                dve.tensor_tensor(hidden[:, s, c, :, :], ps_a[c][:, :, :], hid_s[:, c, :, :], ALU.max).then_inc(s_hid, 1)

            def add_up(g, blk):
                dve.wait_ge(s_seg, g + 1)
                if isinstance(g, int) and g < 1:
                    dve.wait_ge(s_clear, 1)
                else:
                    dve.wait_ge(s_acc, g)
                row = acc[:, bass.ds(blk, 1), :].rearrange("p b r -> p (b r)")
                dve.tensor_tensor(row, row, ps_s[:, :], ALU.add).then_inc(s_acc, 1)

            def step(i, u, left=4):
                g = i * SLOTS + u
                s = u % 2
                early = isinstance(g, int) and g < 2
                if not early:
                    blk = dve.value_load(blk_row[0:1, bass.ds(g - 2, 1)], min_val=0, max_val=BLOCKS)
                if left > 3:
                    compare(g + 3, i + (u + 3) // SLOTS, (u + 3) % SLOTS)
                if left > 1:
                    leaky(g + 1, 1 - s, 0)
                if not early:
                    dve.wait_ge(s_seg, g - 1)
                dve.tensor_tensor(leave[:, s, :, :], iota_row[:, :].unsqueeze(1).to_broadcast([P, TILES, P]),
                                  splace[:, bass.ds(g * TILES, TILES)].unsqueeze(2).to_broadcast([P, TILES, P]),
                                  ALU.is_equal).then_inc(s_leave, 1)
                if not early:
                    add_up(g - 2, blk)
                if left > 1:
                    leaky(g + 1, 1 - s, 1)
                    leaky(g + 1, 1 - s, 2)
                dve.wait_ge(s_alphas, g + 1)
                dve.tensor_tensor(alpha[:, s, :, :], ps_g[:, :, :], alpha_s[:, :, :], ALU.max).then_inc(s_alpha, 1)
                dve.wait_ge(s_expa, g + 1)
                dve.tensor_tensor(vals[:, s, :, VALS:VALS + HEADS], expa[:, s, :, :],
                                  rows[:, u, :, D:HROW].to_broadcast([P, TILES, HEADS]),
                                  ALU.mult).then_inc(s_wgt, 1)
                dve.wait_ge(s_betas, g + 1)
                if not early:
                    dve.wait_ge(s_vals, g - 1)
                dve.tensor_tensor(beta[:, s, :, :], ps_b[:, :, :], beta_s[:, :, :], ALU.max).then_inc(s_beta, 1)

            for g in range(3):
                compare(g, 0, g)
            for c in range(PAIRS):
                leaky(0, 0, c)
            for u in range(SLOTS):
                step(0, u)
            with dve.Fori(1, BODIES - 1) as i:
                for u in range(SLOTS):
                    step(i, u)
            for u in range(SLOTS):
                step(BODIES - 1, u, left=SLOTS - u)
            for g in range(GROUPS - 2, GROUPS):
                add_up(g, dve.value_load(blk_row[0:1, g:g + 1], min_val=0, max_val=BLOCKS))

            dve.wait_ge(s_acc, GROUPS)
            sums = acc[:, 0:BLOCKS, VALS:VALS + HEADS]
            link(dve.tensor_scalar(empty[:, :], acc[:, 0:BLOCKS, VROW - 1:VROW].rearrange("p b o -> p (b o)"),
                                   0.0, None, ALU.is_equal))
            link(dve.tensor_tensor(inv[:, 0, :, :], sums, empty[:, :].unsqueeze(2).to_broadcast([P, BLOCKS, HEADS]),
                                   ALU.add))
            link(dve.reciprocal(inv[:, 1, :, :], inv[:, 0, :, :]))
            link(dve.tensor_scalar(inv[:, 2, :, :], inv[:, 1, :, :], 1e-16, None, ALU.add))
            for h in range(HEADS):
                part = acc[:, 0:BLOCKS, h * D:(h + 1) * D]
                link(dve.tensor_tensor(part, part, inv[:, 2, :, h:h + 1].to_broadcast([P, BLOCKS, D]), ALU.mult))
            for h in (0, 2):
                link(dve.tensor_tensor(acc[:, 0:BLOCKS, h * D:(h + 1) * D], acc[:, 0:BLOCKS, h * D:(h + 1) * D],
                                       acc[:, 0:BLOCKS, (h + 1) * D:(h + 2) * D], ALU.add))
            link(dve.tensor_tensor(xc[:, :, :], acc[:, 0:BLOCKS, 0:D], acc[:, 0:BLOCKS, 2 * D:3 * D], ALU.add))
            dve.scalar_tensor_tensor(xc[:, :, :].rearrange("p b d -> p (b d)"), xc[:, :, :].rearrange("p b d -> p (b d)"),
                                     1.0 / HEADS, xs[:, :, :].rearrange("p b d -> p (b d)"),
                                     ALU.mult, ALU.add).then_inc(s_final, 1)

        @block.tensor
        def _(pe):
            pe.wait_ge(s_const, N_CONST)
            pe.wait_ge(s_xin, 16 * N_XIN)
            pe.transpose(ps_pos, pos_rows[:, :], ident[0:64, 0:64]).then_inc(s_wt, 1)
            pe.wait_ge(s_win, 16 * (N_WIN + HEADS))
            for c in range(PAIRS):
                for k in range(2):
                    last = pe.transpose(ps_w[c][:, k, :], w1[:, 2 * c + k, :], ident[:, :])
                last.then_inc(s_wt, 1)
            for k in range(2):
                last = pe.transpose(ps_x[:, 0, k * P:(k + 1) * P], w2[:, k, :], ident[:, :])
            last.then_inc(s_wt, 1)
            pe.wait_ge(s_count, 1)
            pe.matmul(ps_s[:, 0:BUCKETS], before[:, :], count[:, :], start=True, stop=True)
            pe.matmul(ps_s[:, BUCKETS:2 * BUCKETS], ones[:, :], count[:, :], start=True, stop=True).then_inc(s_pref, 1)
            pe.wait_ge(s_past, 1)
            pe.wait_ge(s_wcopy, 1)
            for k in range(2):
                last = pe.matmul(ps_a_flat[k][:, 0:GROUPS // 2], real[:, :],
                                 iota_group[:, k * (GROUPS // 2):(k + 1) * (GROUPS // 2)], start=True, stop=True)
            last.then_inc(s_blkp, 1)
            pe.wait_ge(s_place, 2)
            for k in range(8):
                last = pe.transpose(ps_t[:, k, :], splace_b[:, k * P:(k + 1) * P], ident_b[:, :])
            last.then_inc(s_pt, 1)
            pe.wait_ge(s_ptc, 1)
            for k in range(TC - 8):
                last = pe.transpose(ps_t[:, k, :], splace_b[:, (k + 8) * P:(k + 9) * P], ident_b[:, :])
            last.then_inc(s_pt, 1)

            def features(g, i, u):
                pe.wait_ge(s_pick, g + 1)
                pe.wait_ge(s_rows[u], (i + 1) * 32)
                if not (isinstance(g, int) and g < 1):
                    pe.wait_ge(s_feat, g)
                for part in range(2):
                    cols = slice(part * D, (part + 1) * D)
                    pe.matmul(ps_x[0:D, part, :], hblk[:, u, :].bitcast(F16)[:, cols], pick[:, u % 2, :], start=True, stop=True)
                    for t in range(TILES):
                        last = pe.matmul(ps_x[D:P, part, t * P:(t + 1) * P], rows[:, u, t, 0:D].bitcast(F16)[:, cols], ident_h[:, :],
                                         start=True, stop=True)
                last.then_inc(s_x, 1)

            def layer1(g, s):
                pe.wait_ge(s_feat, g + 1)
                for c in range(PAIRS):
                    if not (isinstance(g, int) and g < 1):
                        pe.wait_ge(s_hid, g * PAIRS + (c - PAIRS + 1))
                    for k in range(2):
                        o = ps_a[c][:, k, :]
                        pe.matmul(o, w1_hi[:, 2 * c + k, :], feat[:, s, 0, :], start=True, stop=False)
                        pe.matmul(o, w1_hi[:, 2 * c + k, :], feat[:, s, 1, :], start=False, stop=False)
                        last = pe.matmul(o, w1_lo[:, 2 * c + k, :], feat[:, s, 0, :], start=False, stop=True)
                    last.then_inc(s_l1, 1)

            def layer2(g, s):
                pe.wait_ge(s_hid, g * PAIRS + 1)
                if not (isinstance(g, int) and g < 1):
                    pe.wait_ge(s_alpha, g)
                for t in range(TILES):
                    for k in range(2):
                        last = pe.matmul(ps_g[:, t, :], hidden[:, s, 0, k, t * P:(t + 1) * P], gw2s[:, k, :],
                                         start=(k == 0), stop=(k == 1))
                last.then_inc(s_gate, 1)
                if not (isinstance(g, int) and g < 1):
                    pe.wait_ge(s_beta, g)
                for h in range(HEADS):
                    if h % 2 == 0:
                        pe.wait_ge(s_hid, g * PAIRS + (h // 2 + 2))
                    for t in range(TILES):
                        last = pe.matmul(ps_b[:, t, h * D:(h + 1) * D],
                                         hidden[:, s, 1 + h // 2, h % 2, t * P:(t + 1) * P], w2t[:, h, :],
                                         start=True, stop=True)
                last.then_inc(s_l2, 1)

            def segment(g, s):
                pe.wait_ge(s_leave, g + 1)
                pe.wait_ge(s_vals, g + 1)
                if not (isinstance(g, int) and g < 1):
                    pe.wait_ge(s_acc, g)
                for t in range(TILES):
                    last = pe.matmul(ps_s[:, :], leave[:, s, t, :], vals[:, s, t, :],
                                     start=(t == 0), stop=(t == TILES - 1))
                last.then_inc(s_seg, 1)

            def step(i, u, left=3):
                g = i * SLOTS + u
                if left > 2:
                    features(g + 2, i + (u + 2) // SLOTS, (u + 2) % SLOTS)
                if left > 1:
                    layer1(g + 1, (u + 1) % 2)
                layer2(g, u % 2)
                if not (isinstance(g, int) and g < 1):
                    segment(g - 1, (u - 1) % 2)

            pe.wait_ge(s_wcopy, 1)
            features(0, 0, 0)
            features(1, 0, 1)
            layer1(0, 0)
            for u in range(SLOTS):
                step(0, u)
            with pe.Fori(1, BODIES - 1) as i:
                for u in range(SLOTS):
                    step(i, u)
            for u in range(SLOTS):
                step(BODIES - 1, u, left=SLOTS - u)
            segment(GROUPS - 1, (SLOTS - 1) % 2)


_INS = ['x', 'src', 'dst', 'node_vec', 'L0_gnn_gate_w1', 'L0_gnn_gate_w2', 'L0_gnn_msg_w1', 'L0_gnn_msg_w2']
_OUTS = [((6250, 64), 'float32')]


def kernel(**inputs):
    import numpy as _np
    import concourse.bacc as _bacc
    from concourse import mybir as _mybir
    from concourse.bass_utils import run_bass_kernel_spmd as _run

    nc = _bacc.Bacc("TRN2", target_bir_lowering=False, num_devices=1)
    arrays, args = {}, []
    for name in _INS:
        a = _np.ascontiguousarray(inputs[name])
        arrays[f"in_{name}_dram"] = a
        args.append(nc.dram_tensor(f"in_{name}_dram", a.shape, _mybir.dt.from_np(a.dtype), kind="ExternalInput").ap())
    for i, (shape, dtype) in enumerate(_OUTS):
        dt = _mybir.dt.from_np(_np.dtype(dtype))
        args.append(nc.dram_tensor(f"out_{i}_dram", shape, dt, kind="ExternalOutput").ap())
    gnn_preln_kernel(nc, *args)
    r = _run(nc, [arrays], core_ids=[0])
    got = tuple(r.results[0][f"out_{i}_dram"] for i in range(len(_OUTS)))
    return got[0]
```

```python
from contextlib import ExitStack

import concourse.bass as bass
from concourse import mybir

F32 = mybir.dt.float32
F16 = mybir.dt.float16
F32R = mybir.dt.float32r
BF16 = mybir.dt.bfloat16
I32 = mybir.dt.int32
ALU = mybir.AluOpType
ACT = mybir.ActivationFunctionType
AX = mybir.AxisListType
RMAX = bass.bass_isa.ReduceOp.max

P = 128
NEG_SLOPE = 0.2
EPS = 1e-5
GROUP = 256
TILES = GROUP // P
SLOTS = 6
BATCH = 8
LATE_BATCH = SLOTS
NJ_EARLY = 608
PAD_KEY = 255


def gnn_preln_kernel(nc, x, src, dst, node_vec, gate_w1, gate_w2, msg_w1, msg_w2, out):
    N, D = x.shape
    E = src.shape[0]
    HEADS, G_HID, _ = msg_w1.shape
    F_HID = gate_w1.shape[1]
    assert D == 64 and G_HID == P and F_HID == 64 and HEADS == 4

    BLOCKS = -(-N // P)
    LAST = N - (BLOCKS - 1) * P
    BUCKETS = BLOCKS + 1
    NJ = -(-E // P)
    NJ += -NJ % (2 * BATCH)
    NJ_LATE = NJ - NJ_EARLY
    FULL = E // NJ
    REST = E - FULL * NJ
    GROUPS = (P * NJ + BUCKETS * (GROUP - 1)) // GROUP
    GROUPS += -GROUPS % SLOTS
    BODIES = GROUPS // SLOTS
    T = GROUPS * TILES
    TC = -(-T // P)
    RUN_1 = (P * NJ_EARLY - BUCKETS * (GROUP - 1)) // GROUP // SLOTS
    COLS_1 = NJ_EARLY + (RUN_1 - 1) * 2 * LATE_BATCH
    RUN_2 = RUN_1 + (NJ - COLS_1) // (2 * LATE_BATCH) + 1
    COLS = (0, NJ_EARLY, COLS_1, NJ)
    RUNS = (0, RUN_1, RUN_2, BODIES)
    TILE = tuple(r * SLOTS * TILES for r in RUNS)
    SHARED = 3 * BUCKETS // 5
    HID_CHUNKS = (HEADS * F_HID + HEADS * G_HID) // P
    PAIRS = HID_CHUNKS // 2
    VALS = HEADS * D
    VROW = VALS + HEADS + 1
    VCOLS = VROW + VROW % 2
    HROW = D + 1
    assert (NJ - COLS_1) % (2 * LATE_BATCH) == 0
    assert RUN_2 * SLOTS <= (P * COLS_1 - BUCKETS * (GROUP - 1)) // GROUP
    assert NJ_EARLY % (2 * BATCH) == 0 and NJ_EARLY // (2 * BATCH) > BUCKETS // 2 + 1
    assert 2 * BUCKETS <= P and all(-(-TILE[r + 1] // P) - TILE[r] // P <= 8 for r in range(3))
    assert FULL == P - 1 and BUCKETS <= F_HID and D * 2 == P

    key_d = nc.dram_tensor("key_d", [P, T], I32).ap()
    key_flat = key_d.rearrange("p (t o) -> (p t) o", o=1)
    place_d = nc.dram_tensor("place_d", [TC * P, P], BF16).ap()
    place_flat = place_d.rearrange("t p -> (t p)")
    node_d = nc.dram_tensor("node_d", [BUCKETS * P, HROW], F32).ap()

    with ExitStack() as ctx:
        def sb(name, shape, dt):
            return ctx.enter_context(nc.sbuf_tensor(name, shape, dt))

        def ps(name, shape, dt=F32):
            return ctx.enter_context(nc.psum_tensor(name, shape, dt))

        def sem(name):
            return ctx.enter_context(nc.semaphore(name))

        ident = sb("ident", [P, P], F32)
        ident_h = sb("ident_h", [P, P], F16)
        ident_b = sb("ident_b", [P, P], BF16)
        before = sb("before", [P, P], F32)
        steps = sb("steps", [P, P], F32)
        steps_3 = sb("steps_3", [P, P], F32)
        ones = sb("ones", [P, P], F32)
        iota_row = sb("iota_row", [P, P], F32)
        iota_col = sb("iota_col", [P, 1], F32)
        iota_group = sb("iota_group", [P, GROUPS], F32)
        xs = sb("xs", [P, BLOCKS, D], F32)
        xc = sb("xc", [P, BLOCKS, D], F32)
        node = sb("node", [P, BUCKETS, HROW], F32)
        node_h = node[:, 0:BLOCKS, 0:D].bitcast(F16)
        stat = sb("stat", [P, 6, BLOCKS], F32)
        pos_rows = sb("pos_rows", [64, P], F32)
        w1 = sb("w1", [P, HID_CHUNKS, P], F32)
        w1_hi = sb("w1_hi", [P, HID_CHUNKS, P], F16)
        w1_lo = sb("w1_lo", [P, HID_CHUNKS, P], F16)
        w2 = sb("w2", [P, 2, P], F32)
        w2t = sb("w2t", [P, VALS + 2 * HEADS], F32)
        w2_hi = sb("w2_hi", [P, VALS + 2 * HEADS], F16)
        w2_lo = sb("w2_lo", [P, VALS + 2 * HEADS], F16)
        lin = sb("lin", [P, VALS + HEADS], F32)
        lin_hi = sb("lin_hi", [P, VALS + HEADS], F16)
        lin_lo = sb("lin_lo", [P, VALS + HEADS], F16)
        w_top = sb("w_top", [P, 3], F32)
        w_low = sb("w_low", [P, 3], F32)
        w_abs = sb("w_abs", [P, 3], F32)
        w_all = sb("w_all", [P, 3], F32)
        w_exp = sb("w_exp", [P, 3], I32)
        w_expf = sb("w_expf", [P, 3], F32)
        power = sb("power", [P, 7], I32)
        acc = sb("acc", [P, BUCKETS, VROW], F32)
        work = acc[:, :, :].rearrange("p b r -> p (b r)")[:, 0:8 * NJ].rearrange("p (k j) -> p k j", j=NJ)
        h32 = work[:, 6:8, :].rearrange("p k j -> p (k j)")[:, 0:BLOCKS * D].rearrange("p (b d) -> p b d", d=D)
        mask = sb("mask", [P, NJ], BF16)
        src_i, blk_i, rank_p, rank_t = (work[:, k, :].bitcast(I32) for k in range(4))
        cum, rank, picked = work[:, 4, :], work[:, 5, :], work[:, 6:8, :]
        masks = [mask[:, 0:NJ_EARLY], work[:, 0, :].bitcast(BF16)[:, 0:NJ_EARLY]]
        cums = [work[:, k, 0:NJ_EARLY] for k in (4, 2)]
        moves = [work[:, k, 0:NJ_EARLY] for k in (1, 3)]
        moves_2 = [work[:, k, NJ_EARLY:2 * NJ_EARLY] for k in (1, 3)]
        squares = mask[:, NJ_EARLY:2 * NJ_EARLY]
        moved_late = work[:, 1, 0:COLS_1 - NJ_EARLY]
        count_mask = work[:, 3, :].bitcast(BF16)[:, 0:NJ_LATE]
        past_3 = work[:, 0, 0:GROUPS]
        dst_i = sb("dst_i", [P, NJ], I32)
        blk_b = sb("blk_b", [P, NJ], BF16)
        ones_b = sb("ones_b", [P, NJ], BF16)
        bias = sb("bias", [P, 1], F32)
        sign_sum = sb("sign_sum", [P, 3, BUCKETS + 1], F32)
        count = sb("count", [P, 3, BUCKETS], F32)
        grp_i = sb("grp_i", [P, BUCKETS], I32)
        full = sb("full", [P, 2, BUCKETS], F32)
        groups = sb("groups", [P, BUCKETS], F32)
        at = sb("at", [P, 3, BUCKETS], F32)
        ends = sb("ends", [P, P], F32)
        ends_3 = sb("ends_3", [P, BUCKETS], F32)
        w1_flat = w1[:, :, :].rearrange("p c e -> p (c e)")
        totals = w1_flat[:, 0:6 * BUCKETS].rearrange("p (k b) -> p k b", b=BUCKETS)
        early_tab = w1_flat[:, 6 * BUCKETS:11 * BUCKETS].rearrange("p (b k) -> p b k", k=5)
        late_tab = w1_flat[:, 11 * BUCKETS:15 * BUCKETS].rearrange("p (b k) -> p b k", k=4)
        end_col = sb("end_col", [P, 1], F32)
        end_col_3 = sb("end_col_3", [P, 1], F32)
        blk_row = sb("blk_row", [P, GROUPS], I32)
        bucket = sb("bucket", [P, 1], F32)
        bucket_l = sb("bucket_l", [P, 1], F32)
        bucket_c = sb("bucket_c", [P, 1], F32)
        cur = sb("cur", [P, 5], F32)
        cur_l = sb("cur_l", [P, 4], F32)
        sign_out = mask[:, :]
        rank_i = sb("rank_i", [P, NJ], I32)
        stage_key = sb("stage_key", [P, 2, BATCH], I32)
        stage_addr = sb("stage_addr", [P, 2, BATCH], I32)
        skey = sb("skey", [P, T], I32)
        sdst = sb("sdst", [P, T], I32)
        splace = sb("splace", [P, T], F32)
        splace_b = sb("splace_b", [P, TC * P], BF16)
        place_t = sb("place_t", [P, TC, P], BF16)
        idx = sb("idx", [P, SLOTS, TILES], I32)
        rows = sb("rows", [P, SLOTS, TILES, HROW], F32)
        place_bc = sb("place_bc", [P, SLOTS, GROUP], BF16)
        hblk = sb("hblk", [P, SLOTS, D], F32)
        pick = sb("pick", [P, 2, GROUP], F16)
        feat = sb("feat", [P, 3, 2, GROUP], F16)
        hid_hi = sb("hid_hi", [P, 2, PAIRS, 2, GROUP], F16)
        expa = sb("expa", [P, 2, TILES, HEADS], F32)
        hid_lo = sb("hid_lo", [P, 2, PAIRS, 2, GROUP], F16)
        scaled = sb("scaled", [P, TILES, VALS + HEADS], F32)
        beta = sb("beta", [P, 2, TILES, VALS + HEADS], F32)
        vals = sb("vals", [P, 2, TILES, VCOLS], F32)
        vals_hi = sb("vals_hi", [P, 2, TILES, VCOLS], F32R)
        vals_lo = sb("vals_lo", [P, 2, TILES, VCOLS], F32R)
        leave = sb("leave", [P, 2, TILES, P], F32R)
        apart = mask[:, 0:2 * TILES * P].bitcast(F32).rearrange("p (t n) -> p t n", n=P)
        inv = skey[:, 0:3 * BLOCKS * HEADS].bitcast(F32).rearrange("p (k b h) -> p k b h", b=BLOCKS, h=HEADS)
        empty = skey[:, 3 * BLOCKS * HEADS:(3 * HEADS + 1) * BLOCKS].bitcast(F32)

        ps_a = [ps(f"ps_a{c}", [P, 2, GROUP]) for c in range(PAIRS)]
        ps_x = ps("ps_x", [P, 2, GROUP])
        ps_b = ps("ps_b", [P, TILES, 512])
        ps_s_bank = ps("ps_s", [P, 512])
        ps_s = ps_s_bank[:, 0:VCOLS]
        ps_t = ps("ps_t", [P, 8, P], BF16)

        ps_pos = ps_b[:, 0, 0:64]
        ps_a_flat = [ps_a[c][:, :, :].rearrange("p a g -> p (a g)") for c in range(PAIRS)]
        ps_w = [ps_a[c][:, 0, :].rearrange("p (a e) -> p a e", a=2) for c in range(PAIRS)]

        s_const = sem("s_const")
        s_pre = sem("s_pre")
        s_xin = sem("s_xin")
        s_win = sem("s_win")
        s_ein = sem("s_ein")
        s_pad = sem("s_pad")
        s_v = sem("s_v")
        s_var = sem("s_var")
        s_std = sem("s_std")
        s_wt = sem("s_wt")
        s_wmax = sem("s_wmax")
        s_wmaxa = sem("s_wmaxa")
        s_wcopy = sem("s_wcopy")
        s_lin = sem("s_lin")
        s_node = sem("s_node")
        s_nout = sem("s_nout")
        s_blk = sem("s_blk")
        s_bias = sem("s_bias")
        s_sign = sem("s_sign")
        s_count = sem("s_count")
        s_pref = sem("s_pref")
        s_past = sem("s_past")
        s_blkp = sem("s_blkp")
        s_blkrow = sem("s_blkrow")
        s_first = sem("s_first")
        s_square = sem("s_square")
        s_mask = sem("s_mask")
        s_cum = sem("s_cum")
        s_picked = sem("s_picked")
        s_rank = sem("s_rank")
        s_staged = sem("s_staged")
        s_seen = sem("s_seen")
        s_scat = [sem(f"s_scat{u}") for u in range(2)]
        s_latep = sem("s_latep")
        s_lstaged = sem("s_lstaged")
        s_late = [sem(f"s_late{u}") for u in range(2)]
        s_moved = sem("s_moved")
        s_summed = sem("s_summed")
        s_tally = sem("s_tally")
        s_skey = sem("s_skey")
        s_place = sem("s_place")
        s_pt = sem("s_pt")
        s_ptc = sem("s_ptc")
        s_pout = sem("s_pout")
        s_idx = sem("s_idx")
        s_rows = [sem(f"s_rows{u}") for u in range(SLOTS)]
        s_in = [sem(f"s_in{u}") for u in range(SLOTS)]
        s_pick = sem("s_pick")
        s_x = sem("s_x")
        s_feat = sem("s_feat")
        s_l1 = sem("s_l1")
        s_hid = sem("s_hid")
        s_hids = sem("s_hids")
        s_scaled = sem("s_scaled")
        s_expa = sem("s_expa")
        s_l2 = sem("s_l2")
        s_beta = sem("s_beta")
        s_wgt = sem("s_wgt")
        s_weighed = sem("s_weighed")
        s_high = sem("s_high")
        s_vals = sem("s_vals")
        s_leave = sem("s_leave")
        s_apart = sem("s_apart")
        s_seg = sem("s_seg")
        s_acc = sem("s_acc")
        s_clear = sem("s_clear")
        s_final = sem("s_final")
        s_out = sem("s_out")

        block = ctx.enter_context(nc.Block())

        N_CONST = 14
        N_XIN = 4
        N_WIN = 6

        @block.sync
        def _(sp):
            sp.wait_ge(s_pre, 2)
            sp.dma_start(src_i[0:FULL, :], src[0:FULL * NJ].rearrange("(p j) -> p j", j=NJ)).then_inc(s_ein, 16)
            sp.dma_start(src_i[FULL:FULL + 1, 0:REST], src[FULL * NJ:E].rearrange("(p j) -> p j", p=1)).then_inc(s_ein, 16)
            sp.dma_start(dst_i[0:FULL, :], dst[0:FULL * NJ].rearrange("(p j) -> p j", j=NJ)).then_inc(s_ein, 16)
            sp.dma_start(dst_i[FULL:FULL + 1, 0:REST], dst[FULL * NJ:E].rearrange("(p j) -> p j", p=1)).then_inc(s_ein, 16)
            sp.wait_ge(s_pre, 5)
            sp.dma_start(xs[:, 0:BLOCKS - 1, :],
                         x[0:(BLOCKS - 1) * P, :].rearrange("(b p) d -> p b d", p=P)).then_inc(s_xin, 16)
            sp.dma_start(xs[0:LAST, BLOCKS - 1, :], x[(BLOCKS - 1) * P:N, :]).then_inc(s_xin, 16)
            sp.dma_start(pos_rows[0:BLOCKS - 1, :],
                         node_vec[0:(BLOCKS - 1) * P].rearrange("(b p) -> b p", p=P)).then_inc(s_xin, 16)
            sp.dma_start(pos_rows[BLOCKS - 1:BLOCKS, 0:LAST],
                         node_vec[(BLOCKS - 1) * P:N].rearrange("(b p) -> b p", b=1)).then_inc(s_xin, 16)
            sp.dma_start(w1[:, 0:2, :], gate_w1.rearrange("(c a) f e -> (a f) c e", a=2)).then_inc(s_win, 16)
            sp.dma_start(w1[:, 2:2 + HEADS, :], msg_w1.rearrange("h f e -> f h e")).then_inc(s_win, 16)
            for h in range(HEADS):
                sp.dma_start(w2[(h % 2) * D:(h % 2 + 1) * D, h // 2, :], msg_w2[h, :, :]).then_inc(s_win, 16)
            sp.dma_start(key_d, skey[:, :]).then_inc(s_pad, 16)
            sp.wait_ge(s_node, 1)
            sp.dma_start(node_d.rearrange("(b p) r -> p b r", p=P), node[:, :, :]).then_inc(s_nout, 16)
            for u in range(2):
                sp.wait_ge(s_scat[u], 16 * NJ_EARLY // 2)
            sp.dma_start(skey[:, 0:TILE[1]], key_d[:, 0:TILE[1]]).then_inc(s_skey, 16)
            sp.wait_ge(s_ptc, 1)
            blocks = -(-TILE[1] // P)
            sp.dma_start(place_d[0:blocks * P, :].rearrange("(a t) p -> t a p", t=P),
                         place_t[:, 0:blocks, :]).then_inc(s_pout, 16)
            places_out = 16
            sp.wait_ge(s_pout, places_out)
            sp.wait_ge(s_nout, 16)
            sp.wait_ge(s_blkrow, 1)

            def load(g, i, u):
                blk = sp.value_load(blk_row[0:1, bass.ds(g, 1)], min_val=0, max_val=BLOCKS)
                if not (isinstance(g, int) and g < SLOTS):
                    sp.wait_ge(s_x, g - SLOTS + 1)
                    sp.wait_ge(s_pick, g - SLOTS + 1)
                sp.dma_start(hblk[:, u, :], node_d[bass.ds(blk * P, P), 0:D]).then_inc(s_in[u], 16)
                sp.dma_start(place_bc[:, u, :],
                             place_flat[bass.ds(g * GROUP, GROUP)].rearrange("(o n) -> o n", o=1)
                             .to_broadcast([P, GROUP])).then_inc(s_in[u], 16)

            for u in range(SLOTS):
                load(u, 0, u)
            for r in range(3):
                with sp.Fori(max(RUNS[r], 1), RUNS[r + 1]) as i:
                    for u in range(SLOTS):
                        load(i * SLOTS + u, i, u)
                if r < 2:
                    for u in range(2):
                        sp.wait_ge(s_late[u], (RUNS[r + 1] - 1 - r) * 16 * LATE_BATCH)
                    a, z = TILE[r + 1:r + 3]
                    sp.dma_start(skey[:, a:z], key_d[:, a:z]).then_inc(s_skey, 16)
                    sp.wait_ge(s_ptc, r + 2)
                    if a % P:
                        sp.dma_start(place_d[a:a + P - a % P, :], place_t[a % P:P, a // P, :]).then_inc(s_pout, 16)
                        places_out += 16
                    k, end = -(-a // P), -(-z // P)
                    sp.dma_start(place_d[k * P:end * P, :].rearrange("(a t) p -> t a p", t=P),
                                 place_t[:, k:end, :]).then_inc(s_pout, 16)
                    places_out += 16
                    sp.wait_ge(s_pout, places_out)
            sp.wait_ge(s_final, 1)
            sp.dma_start(out[0:(BLOCKS - 1) * P, :].rearrange("(b p) d -> p b d", p=P),
                         xc[:, 0:BLOCKS - 1, :]).then_inc(s_out, 16)
            sp.dma_start(out[(BLOCKS - 1) * P:N, :], xc[0:LAST, BLOCKS - 1, :]).then_inc(s_out, 16)
            sp.wait_ge(s_out, 32)

        @block.gpsimd
        def _(pool):
            pool.memset(ident[:, :], 0.0).then_inc(s_const, 1)
            pool.memset(ones[:, :], 1.0).then_inc(s_const, 1)
            pool.iota(iota_row[:, :], pattern=[[1, P]], base=0, channel_multiplier=0,
                      allow_small_or_imprecise_dtypes=True).then_inc(s_const, 1)
            pool.iota(iota_col[:, :], pattern=[[1, 1]], base=0, channel_multiplier=1,
                      allow_small_or_imprecise_dtypes=True).then_inc(s_const, 1)
            pool.iota(iota_group[:, :], pattern=[[1, GROUPS]], base=0, channel_multiplier=0,
                      allow_small_or_imprecise_dtypes=True).then_inc(s_const, 1)
            pool.wait_ge(s_const, 5)
            pool.affine_select(out=ident[:, :], in_=ident[:, :], compare_op=ALU.not_equal, fill=1.0,
                               base=0, pattern=[[-1, P]], channel_multiplier=1).then_inc(s_const, 1)
            pool.affine_select(out=before[:, :], in_=ones[:, :], compare_op=ALU.is_gt, fill=0.0,
                               base=0, pattern=[[1, P]], channel_multiplier=-1).then_inc(s_const, 1)
            pool.affine_select(out=steps[:, :], in_=ones[:, :], compare_op=ALU.is_gt, fill=0.0,
                               base=2 * BUCKETS, pattern=[[0, P]], channel_multiplier=-1).then_inc(s_const, 1)
            pool.affine_select(out=steps_3[:, :], in_=ones[:, :], compare_op=ALU.is_gt, fill=0.0,
                               base=BLOCKS, pattern=[[0, P]], channel_multiplier=-1).then_inc(s_const, 1)
            pool.wait_ge(s_const, 9)
            pool.tensor_copy(ident_h[:, :], ident[:, :]).then_inc(s_const, 1)
            pool.tensor_copy(ident_b[:, :], ident[:, :]).then_inc(s_const, 1)
            pool.memset(rank[:, :], 0.0).then_inc(s_const, 1)
            pool.affine_select(out=steps[:, :], in_=steps[:, :], compare_op=ALU.not_equal, fill=-float(BLOCKS),
                               base=-BLOCKS, pattern=[[0, P]], channel_multiplier=1).then_inc(s_const, 1)
            pool.wait_ge(s_const, N_CONST - 1)
            pool.affine_select(out=steps[:, :], in_=steps[:, :], compare_op=ALU.not_equal, fill=-float(BLOCKS),
                               base=-(BUCKETS + BLOCKS), pattern=[[0, P]], channel_multiplier=1).then_inc(s_const, 1)
            pool.wait_ge(s_wmax, 1)
            pool.partition_all_reduce(w_all[:, :], w_abs[:, :], P, RMAX).then_inc(s_wmaxa, 1)
            pool.wait_ge(s_const, N_CONST)

            def add_places(b, u):
                pool.wait_ge(s_moved, 3 * b + 3)
                pool.tensor_tensor(moves[u], moves[u], cums[u], ALU.add).then_inc(s_summed, 1)
                if not (isinstance(b, int) and b < 2):
                    add_picked(b - 2, u)

            def add_picked(b, u):
                pool.wait_ge(s_picked, b + 1)
                if not (isinstance(b, int) and b < 1):
                    pool.wait_ge(s_rank, b)
                pool.tensor_tensor(rank[:, 0:NJ_EARLY], rank[:, 0:NJ_EARLY], picked[:, u, 0:NJ_EARLY],
                                   ALU.add).then_inc(s_rank, 1)

            for b in range(4):
                add_places(b, b % 2)
            with pool.Fori(2, BUCKETS // 2) as b2:
                for u in range(2):
                    add_places(b2 * 2 + u, u)
            for b in range(BUCKETS - 2, BUCKETS):
                add_picked(b, b % 2)

            pool.wait_ge(s_pad, 16)

            def scatter(u, a, b, landed):
                for k in range(a, b):
                    pool.indirect_dma_start(
                        out=key_flat, out_offset=bass.IndirectOffsetOnAxis(ap=stage_addr[:, u, k:k + 1], axis=0),
                        in_=stage_key[:, u, k:k + 1], in_offset=None).then_inc(landed[u], 16)

            with pool.Fori(0, NJ_EARLY // (2 * BATCH)) as j:
                for u in range(2):
                    pool.wait_ge(s_staged, j * 4 + (2 * u + 2))
                    pool.sem_inc(s_seen, 1)
                    scatter(u, 0, BATCH, s_scat)

            def late_scatter(n, u):
                if u % (SLOTS // 2) == 0:
                    pool.wait_ge(s_lstaged, n * 4 + (2 if u == 0 else 4))
                    pool.sem_inc(s_seen, 1)
                k = 2 * (u % (SLOTS // 2))
                scatter(u // (SLOTS // 2), k, k + 2, s_late)

            pool.wait_ge(s_place, 1)
            pool.wait_ge(s_nout, 16)

            def gather(g, i, u):
                if not (isinstance(g, int) and g < SLOTS):
                    pool.wait_ge(s_rows[u], i * 32)
                    pool.wait_ge(s_x, g - (SLOTS - 1))
                    pool.wait_ge(s_wgt, g - (SLOTS - 1))
                    pool.sem_inc(s_seen, 1)
                pool.tensor_copy(idx[:, u, :], sdst[:, bass.ds(g * TILES, TILES)]).then_inc(s_idx, 1)
                pool.wait_ge(s_idx, g + 1)
                pool.sem_inc(s_seen, 1)
                for t in range(TILES):
                    pool.indirect_dma_start(
                        out=rows[:, u, t, :], out_offset=None, in_=node_d,
                        in_offset=bass.IndirectOffsetOnAxis(ap=idx[:, u, t:t + 1], axis=0)).then_inc(s_rows[u], 16)

            def weigh(g, s):
                pool.wait_ge(s_wgt, g + 1)
                pool.tensor_tensor(vals[:, s, :, 0:VALS].rearrange("p t (h d) -> p t h d", d=D),
                                   beta[:, s, :, 0:VALS].rearrange("p t (h d) -> p t h d", d=D),
                                   vals[:, s, :, VALS:VALS + HEADS].unsqueeze(3).to_broadcast([P, TILES, HEADS, D]),
                                   ALU.mult).then_inc(s_weighed, 1)

            def body(r, i, first=False, last=False):
                for u in range(SLOTS):
                    g = i * SLOTS + u
                    if u == 0:
                        if not first:
                            gather(g + SLOTS - 1, i, SLOTS - 1)
                    elif not last:
                        gather(g + SLOTS - 1, i + 1, u - 1)
                    if r < 2:
                        if not last:
                            late_scatter(i - r, u)
                    else:
                        weigh(g, u % 2)

            for r in range(3):
                begin, end = RUNS[r:r + 2]
                pool.wait_ge(s_place, 2 * r + 1)
                for u in range(SLOTS):
                    gather(begin * SLOTS + u, begin, u)
                body(r, begin, first=True)
                with pool.Fori(begin + 1, end - 1) as i:
                    body(r, i)
                body(r, end - 1, last=True)

        @block.scalar
        def _(act):
            act.wait_ge(s_pre, 5)
            for h in range(HEADS):
                act.dma_start(w2t[(h % 2) * F_HID:(h % 2 + 1) * F_HID,
                                  VALS + h // 2 * HEADS + h:VALS + h // 2 * HEADS + h + 1],
                              gate_w2[h, :, :].rearrange("o f -> f o")).then_inc(s_win, 16)
            parts = tuple(zip(COLS[:-1], COLS[1:]))
            act.wait_ge(s_blk, 1)

            def signs(b, both):
                for k, (a, z) in enumerate(parts if both else parts[0:1]):
                    act.activation(sign_out[:, a:z], blk_b[:, a:z], ACT.Sign, bias=bias[:, 0:1],
                                   accum_out=sign_sum[:, k, bass.ds(b, 1)]).then_inc(s_sign, 1)

            def count_buckets(begin, end, both):
                with act.Fori(begin, end) as b:
                    act.wait_ge(s_sign, b * 3 if both else b + 2 * (SHARED + 1))
                    act.activation(bias[:, :], bias[:, :], ACT.Copy, bias=-1.0).then_inc(s_bias, 1)
                    act.wait_ge(s_bias, b)
                    signs(b, both)

            signs(0, True)
            count_buckets(1, SHARED // 3, True)
            act.wait_ge(s_var, 1)
            act.activation(stat[:, 3, :], stat[:, 2, :], ACT.Sqrt).then_inc(s_std, 1)
            count_buckets(SHARED // 3, SHARED + 1, True)
            count_buckets(SHARED + 1, BUCKETS, False)

            def bucket_mask(b, u):
                if not (isinstance(b, int) and b < 1):
                    act.wait_ge(s_mask, b)
                    act.wait_ge(s_square, 2 * b)
                act.activation(squares, blk_b[:, 0:NJ_EARLY], ACT.Square, bias=bucket[:, 0:1]).then_inc(s_square, 1)
                act.wait_ge(s_square, 2 * b + 1)
                act.activation(bucket[:, :], bucket[:, :], ACT.Copy, bias=-1.0).then_inc(s_square, 1)
                if not (isinstance(b, int) and b < 2):
                    act.wait_ge(s_picked, b - 1)
                act.activation(masks[u], squares, ACT.Relu, scale=-1.0, bias=1.0).then_inc(s_mask, 1)

            act.wait_ge(s_blkrow, 1)
            for b in range(4):
                bucket_mask(b, b % 2)
            with act.Fori(2, BUCKETS // 2) as b2:
                for u in range(2):
                    bucket_mask(b2 * 2 + u, u)

            def relu(g, s, c):
                act.wait_ge(s_l1, g * PAIRS + c + 1)
                act.activation(hid_hi[:, s, c, :, :], ps_a[c][:, :, :], ACT.Relu).then_inc(s_hids, 1)

            def copy_feat(g, s):
                act.wait_ge(s_x, g + 1)
                act.activation(feat[:, s, :, :], ps_x[:, :, :], ACT.Copy).then_inc(s_feat, 1)

            def high(g, s):
                act.wait_ge(s_weighed, g + 1)
                if not (isinstance(g, int) and g < 2):
                    act.wait_ge(s_seg, g - 1)
                act.activation(vals_hi[:, s, :, :], vals[:, s, :, :], ACT.Copy).then_inc(s_high, 1)

            def exponentials(g, s):
                act.wait_ge(s_beta, g + 1)
                if not (isinstance(g, int) and g < 2):
                    act.wait_ge(s_wgt, g - 1)
                act.activation(expa[:, s, :, :], beta[:, s, :, VALS:VALS + HEADS], ACT.Exp,
                               scale=power[:, 6:7].bitcast(F32)).then_inc(s_expa, 1)

            def leaving(g, s):
                if not (isinstance(g, int) and g < 2):
                    act.wait_ge(s_seg, g - 1)
                    act.wait_ge(s_leave, g)
                for k in range(TILES):
                    act.activation(apart[:, k, :], iota_row[:, :], ACT.Square, scale=-1.0,
                                   bias=splace[:, bass.ds(g * TILES + k, 1)]).then_inc(s_apart, 1)
                act.wait_ge(s_apart, g * TILES + TILES)
                act.activation(leave[:, s, :, :], apart[:, :, :], ACT.Relu, scale=-1.0, bias=1.0).then_inc(s_leave, 1)

            def step(g, u, late, left=3, done=2):
                s = u % 2
                if done > 1:
                    high(g - 2, s)
                if left > 2:
                    copy_feat(g + 2, (u + 2) % 3)
                if left > 1:
                    relu(g + 1, 1 - s, 0)
                if done > 0:
                    exponentials(g - 1, 1 - s)
                if left > 1:
                    relu(g + 1, 1 - s, 1)
                    relu(g + 1, 1 - s, 2)
                if late and done > 0:
                    leaving(g - 1, 1 - s)
                act.wait_ge(s_l2, g + 1)
                if not (isinstance(g, int) and g < 1):
                    act.wait_ge(s_beta, g)
                act.activation(scaled[:, :, :], ps_b[:, :, 0:VALS + HEADS], ACT.Copy,
                               scale=NEG_SLOPE).then_inc(s_scaled, 1)

            def run(begin, end, late):
                g = begin * SLOTS
                copy_feat(g, 0)
                copy_feat(g + 1, 1)
                for c in range(PAIRS):
                    relu(g, 0, c)
                for u in range(SLOTS):
                    step(g + u, u, late, done=u)
                with act.Fori(begin + 1, end - 1) as i:
                    for u in range(SLOTS):
                        step(i * SLOTS + u, u, late)
                for u in range(SLOTS):
                    step((end - 1) * SLOTS + u, u, late, left=SLOTS - u)
                if late:
                    leaving(end * SLOTS - 1, 1)
                high(end * SLOTS - 2, 0)
                exponentials(end * SLOTS - 1, 1)
                high(end * SLOTS - 1, 1)

            act.wait_ge(s_place, 2)
            for r in range(3):
                run(RUNS[r], RUNS[r + 1], late=(r < 2))

        @block.vector
        def _(dve):
            chain = [0]

            def link(ins):
                chain[0] += 1
                ins.then_inc(s_v, 1)
                dve.wait_ge(s_v, chain[0])

            dve.memset(src_i[96:P, :], BLOCKS * P).then_inc(s_pre, 1)
            dve.memset(dst_i[96:P, :], 0).then_inc(s_pre, 1)
            dve.memset(xs[:, BLOCKS - 1, :], 0.0).then_inc(s_pre, 1)
            dve.memset(w2t[:, VALS:], 0.0)
            dve.memset(pos_rows[:, :], 0.0).then_inc(s_pre, 1)
            dve.memset(skey[:, :], PAD_KEY).then_inc(s_pre, 1)
            dve.memset(bucket[:, :], 0.0)
            dve.memset(bucket_l[:, :], 0.0)
            dve.memset(bucket_c[:, :], float(SHARED))
            dve.memset(ends[:, :], 0.0)

            dve.memset(bias[:, :], 0.5)
            dve.wait_ge(s_ein, 64)
            link(dve.tensor_scalar(blk_i[:, :], src_i[:, :], 7, None, ALU.logical_shift_right))
            dve.tensor_copy(blk_b[:, :], blk_i[:, :]).then_inc(s_blk, 1)
            link(dve.tensor_scalar(rank_i[:, :], src_i[:, :], P - 1, None, ALU.bitwise_and))
            link(dve.scalar_tensor_tensor(dst_i[:, :], dst_i[:, :], 256.0, rank_i[:, :], ALU.mult, ALU.add))
            dve.memset(ones_b[:, :], 1.0)
            dve.memset(vals[:, :, :, VROW:VCOLS], 0.0)
            dve.memset(vals[:, :, :, VROW - 1:VROW], 1.0)
            dve.memset(splace_b[:, :], float(PAD_KEY))
            link(dve.memset(node[:, :, :], 0.0))

            dve.wait_ge(s_xin, 16 * N_XIN)
            link(dve.tensor_reduce(stat[:, 0, :], xs[:, :, :], AX.X, ALU.add))
            link(dve.tensor_scalar(stat[:, 1, :], stat[:, 0, :], 1.0 / D, None, ALU.mult))
            link(dve.tensor_tensor(xc[:, :, :], xs[:, :, :],
                                   stat[:, 1, :].unsqueeze(2).to_broadcast([P, BLOCKS, D]), ALU.subtract))
            link(dve.tensor_tensor(h32[:, :, :], xc[:, :, :], xc[:, :, :], ALU.mult))
            link(dve.tensor_reduce(stat[:, 0, :], h32[:, :, :], AX.X, ALU.add))
            dve.tensor_scalar(stat[:, 2, :], stat[:, 0, :], 1.0 / D, EPS, ALU.mult, ALU.add).then_inc(s_var, 1)
            dve.wait_ge(s_std, 1)
            link(dve.reciprocal(stat[:, 4, :], stat[:, 3, :]))
            link(dve.tensor_tensor(xc[:, :, :], xc[:, :, :],
                                   stat[:, 4, :].unsqueeze(2).to_broadcast([P, BLOCKS, D]), ALU.mult))
            link(dve.tensor_scalar(h32[:, :, :], xc[:, :, :], 0.0, None, ALU.max))
            link(dve.tensor_copy(node_h[:, :, 0:D], h32[:, :, :]))
            link(dve.tensor_tensor(node_h[:, :, D:2 * D], h32[:, :, :], node_h[:, :, 0:D], ALU.subtract))
            dve.wait_ge(s_wt, 1)
            dve.tensor_copy(node[:, 0:BLOCKS, D:HROW].rearrange("p b o -> p (b o)"),
                            ps_pos[:, 0:BLOCKS]).then_inc(s_node, 1)

            dve.wait_ge(s_wt, 2 + PAIRS)
            link(dve.tensor_copy(w2t[:, 0:VALS], ps_x[:, 0, :]))
            dve.wait_ge(s_win, 16 * (N_WIN + HEADS))
            weight_sets = (w1[:, :, :].rearrange("p c e -> p (c e)"), w2t[:, 0:VALS], w2t[:, VALS:])
            for k, w in enumerate(weight_sets):
                dve.tensor_reduce(w_low[:, k:k + 1], w, AX.X, ALU.min)
                last = dve.tensor_reduce(w_top[:, k:k + 1], w, AX.X, ALU.max)
            link(last)
            link(dve.tensor_scalar(w_low[:, :], w_low[:, :], -1.0, 1e-17, ALU.mult, ALU.max))
            dve.tensor_tensor(w_abs[:, :], w_top[:, :], w_low[:, :], ALU.max).then_inc(s_wmax, 1)
            dve.wait_ge(s_wmaxa, 1)
            link(dve.tensor_scalar(w_exp[:, :], w_all[:, :].bitcast(I32), 23, None, ALU.logical_shift_right))
            link(dve.tensor_copy(w_expf[:, :], w_exp[:, :]))
            e1 = w_expf[:, 0:1]
            dve.tensor_scalar(power[:, 0:1], e1, -1.0, 134.0 + 127, ALU.mult, ALU.add)
            dve.tensor_scalar(power[:, 1:3], w_expf[:, 1:3], -1.0, 128.0 + 127, ALU.mult, ALU.add)
            link(dve.tensor_scalar(power[:, 5:7], w_expf[:, 1:3], e1, -(134.0 + 128 - 127), ALU.add, ALU.add))
            link(dve.tensor_scalar(power[:, 3:5], power[:, 5:7], -1.0, 254.0, ALU.mult, ALU.add))
            link(dve.tensor_scalar(power[:, :], power[:, :], 23, None, ALU.logical_shift_left))
            pw = power[:, :].bitcast(F32)
            for c in range(PAIRS):
                link(dve.tensor_scalar(w1_hi[:, 2 * c:2 * c + 2, :], ps_w[c], pw[:, 0:1], None, ALU.mult))
                link(dve.scalar_tensor_tensor(w1_lo[:, 2 * c:2 * c + 2, :], ps_w[c], pw[:, 0:1],
                                              w1_hi[:, 2 * c:2 * c + 2, :], ALU.mult, ALU.subtract))
            dve.wait_ge(s_lin, 1)
            for k, (a, b) in enumerate(((0, VALS), (VALS, VALS + HEADS))):
                link(dve.tensor_scalar(lin[:, a:b], ps_b[:, 0, a:b], pw[:, 3 + k:4 + k], NEG_SLOPE, ALU.mult, ALU.mult))
            link(dve.tensor_copy(lin_hi[:, :], lin[:, :]))
            link(dve.tensor_tensor(lin_lo[:, :], lin[:, :], lin_hi[:, :], ALU.subtract))
            for k, (a, b) in enumerate(((0, VALS), (VALS, VALS + 2 * HEADS))):
                link(dve.tensor_scalar(w2t[:, a:b], w2t[:, a:b], pw[:, 1 + k:2 + k], 1.0 - NEG_SLOPE, ALU.mult, ALU.mult))
            link(dve.tensor_copy(w2_hi[:, :], w2t[:, :]))
            dve.tensor_tensor(w2_lo[:, :], w2t[:, :], w2_hi[:, :], ALU.subtract).then_inc(s_wcopy, 1)

            with dve.Fori(0, BUCKETS - SHARED) as b:
                dve.tensor_scalar(count_mask, blk_b[:, NJ_EARLY:NJ], bucket_c[:, 0:1], None,
                                  ALU.is_equal).then_inc(s_tally, 1)
                dve.wait_ge(s_tally, b * 4 + 1)
                for k in (1, 2):
                    dve.tensor_reduce(count[:, k, bass.ds(b + SHARED, 1)],
                                      count_mask[:, COLS[k] - NJ_EARLY:COLS[k + 1] - NJ_EARLY],
                                      AX.X, ALU.add).then_inc(s_tally, 1)
                dve.tensor_scalar(bucket_c[:, :], bucket_c[:, :], 1.0, None, ALU.add).then_inc(s_tally, 1)
                dve.wait_ge(s_tally, b * 4 + 4)
            dve.wait_ge(s_sign, BUCKETS + 2 * (SHARED + 1))
            link(dve.memset(sign_sum[:, 0, BUCKETS:BUCKETS + 1], -float(NJ_EARLY)))
            for k, end in enumerate((BUCKETS, SHARED, SHARED)):
                link(dve.tensor_tensor(count[:, k, 0:end], sign_sum[:, k, 0:end], sign_sum[:, k, 1:end + 1],
                                       ALU.subtract))
                last = dve.tensor_scalar(count[:, k, 0:end], count[:, k, 0:end], 0.5, None, ALU.mult)
            last.then_inc(s_count, 1)
            dve.wait_ge(s_pref, 1)
            link(dve.tensor_copy(w1_flat[:, 0:6 * BUCKETS], ps_s_bank[:, 0:6 * BUCKETS]))
            before_0, before_1, before_2, all_0, all_1, all_2 = (totals[:, k, :] for k in range(6))
            link(dve.tensor_tensor(all_1, all_1, all_0, ALU.add))
            link(dve.tensor_tensor(all_2, all_2, all_1, ALU.add))
            first_group = 0.0
            for k, (edges, scan) in enumerate(((all_0, ends[:, 0:BUCKETS]), (all_1, ends[:, BUCKETS:2 * BUCKETS]),
                                               (all_2, ends_3[:, :]))):
                link(dve.tensor_scalar(grp_i[:, :], edges, float(GROUP - 1 if k == 2 else 0), None, ALU.add))
                link(dve.tensor_scalar(grp_i[:, :], grp_i[:, :], GROUP.bit_length() - 1, None, ALU.logical_shift_right))
                link(dve.tensor_copy(groups[:, :], grp_i[:, :]))
                if k < 2:
                    link(dve.tensor_copy(full[:, k, :], groups[:, :]))
                if k > 0:
                    link(dve.tensor_tensor(groups[:, :], groups[:, :], full[:, k - 1, :], ALU.subtract))
                link(dve.tensor_tensor_scan(scan, ones[:, 0:BUCKETS], groups[:, :], first_group, ALU.mult, ALU.add))
                first_group = scan[:, BUCKETS - 1:BUCKETS]
                link(dve.tensor_tensor(at[:, k, :], scan, groups[:, :], ALU.subtract))
                if k > 0:
                    link(dve.tensor_tensor(at[:, k, :], at[:, k, :], full[:, k - 1, :], ALU.subtract))
                link(dve.tensor_scalar(at[:, k, :], at[:, k, :], float(GROUP), None, ALU.mult))
            link(dve.tensor_tensor(ends[:, :], ends[:, :], ident[:, :], ALU.mult))
            dve.tensor_reduce(end_col[:, :], ends[:, :], AX.X, ALU.add)
            link(dve.tensor_tensor(ends_3[:, :], ends_3[:, :], ident[:, 0:BUCKETS], ALU.mult))
            link(dve.tensor_reduce(end_col_3[:, :], ends_3[:, :], AX.X, ALU.add))
            link(dve.tensor_scalar(past_3, iota_group[:, :], end_col_3[:, 0:1], None, ALU.is_ge))
            dve.tensor_scalar(iota_group[:, :], iota_group[:, :], end_col[:, 0:1], None, ALU.is_ge).then_inc(s_past, 1)
            for k in range(2):
                link(dve.tensor_scalar(full[:, k, :], full[:, k, :], float(GROUP), None, ALU.mult))

            def column(tab, k):
                return tab[:, :, k:k + 1].rearrange("p b o -> p (b o)")

            link(dve.scalar_tensor_tensor(column(early_tab, 0), at[:, 0, :], -1.0, before_0, ALU.add, ALU.add))
            for k in range(2):
                link(dve.tensor_tensor(column(early_tab, 1 + 2 * k), at[:, 0, :], full[:, k, :], ALU.add))
                link(dve.tensor_tensor(column(early_tab, 2 + 2 * k), at[:, k + 1, :], at[:, k, :], ALU.subtract))
            link(dve.scalar_tensor_tensor(column(late_tab, 0), at[:, 1, :], -1.0, before_1, ALU.add, ALU.add))
            link(dve.tensor_tensor(column(late_tab, 0), column(late_tab, 0), all_0, ALU.add))
            link(dve.tensor_tensor(column(late_tab, 1), at[:, 1, :], full[:, 1, :], ALU.add))
            link(dve.tensor_tensor(column(late_tab, 2), at[:, 2, :], at[:, 1, :], ALU.subtract))
            link(dve.scalar_tensor_tensor(column(late_tab, 3), at[:, 2, :], -1.0, before_2, ALU.add, ALU.add))
            link(dve.tensor_tensor(column(late_tab, 3), column(late_tab, 3), all_1, ALU.add))
            dve.wait_ge(s_blkp, 1)
            dve.tensor_copy(blk_row[:, 0:GROUPS // 2], ps_a_flat[0][:, 0:GROUPS // 2])
            dve.tensor_copy(blk_row[:, GROUPS // 2:GROUPS], ps_a_flat[1][:, 0:GROUPS // 2]).then_inc(s_blkrow, 1)

            def pick_places(b, u):
                dve.wait_ge(s_summed, b + 1)
                if not (isinstance(b, int) and b < 2):
                    dve.wait_ge(s_rank, b - 1)
                dve.tensor_tensor(picked[:, u, 0:NJ_EARLY], moves[u], masks[u], ALU.mult).then_inc(s_picked, 1)

            def early_places(b, u):
                dve.tensor_copy(cur[:, :],
                                early_tab[:, bass.ds(b, 1), :].rearrange("p b k -> p (b k)")).then_inc(s_first, 1)
                if not (isinstance(b, int) and b < 2):
                    dve.wait_ge(s_picked, b - 1)
                dve.wait_ge(s_mask, b + 1)
                dve.wait_ge(s_first, b + 1)
                if not (isinstance(b, int) and b < 2):
                    dve.wait_ge(s_summed, b - 1)
                dve.tensor_tensor_scan(cums[u], ones_b[:, 0:NJ_EARLY], masks[u], cur[:, 0:1],
                                       ALU.mult, ALU.add).then_inc(s_cum, 1)
                dve.wait_ge(s_cum, b + 1)
                dve.tensor_scalar(moves[u], cums[u], cur[:, 1:2], cur[:, 2:3],
                                  ALU.is_ge, ALU.mult).then_inc(s_moved, 1)
                dve.tensor_scalar(moves_2[u], cums[u], cur[:, 3:4], cur[:, 4:5],
                                  ALU.is_ge, ALU.mult).then_inc(s_moved, 1)
                if not (isinstance(b, int) and b < 1):
                    pick_places(b - 1, 1 - u)
                dve.wait_ge(s_moved, 3 * b + 2)
                dve.tensor_tensor(moves[u], moves[u], moves_2[u], ALU.add).then_inc(s_moved, 1)
                dve.wait_ge(s_moved, 3 * b + 3)

            for b in range(4):
                early_places(b, b % 2)
            with dve.Fori(2, BUCKETS // 2) as b2:
                for u in range(2):
                    early_places(b2 * 2 + u, u)
            pick_places(BUCKETS - 1, 1)

            def late_places(b):
                cols, part_1, part_2 = (slice(*COLS[1::2]), slice(*COLS[1:3]), slice(*COLS[2:4]))
                dve.tensor_copy(cur_l[:, :],
                                late_tab[:, bass.ds(b, 1), :].rearrange("p b k -> p (b k)")).then_inc(s_latep, 1)
                dve.tensor_scalar(mask[:, cols], blk_b[:, cols], bucket_l[:, 0:1], None, ALU.is_equal).then_inc(s_latep, 1)
                dve.wait_ge(s_latep, b * 9 + 2)
                dve.tensor_tensor_scan(cum[:, part_1], ones_b[:, part_1], mask[:, part_1], cur_l[:, 0:1],
                                       ALU.mult, ALU.add).then_inc(s_latep, 1)
                dve.tensor_tensor_scan(cum[:, part_2], ones_b[:, part_2], mask[:, part_2], cur_l[:, 3:4],
                                       ALU.mult, ALU.add).then_inc(s_latep, 1)
                dve.wait_ge(s_latep, b * 9 + 4)
                dve.tensor_scalar(moved_late, cum[:, part_1], cur_l[:, 1:2], cur_l[:, 2:3],
                                  ALU.is_ge, ALU.mult).then_inc(s_latep, 1)
                dve.wait_ge(s_latep, b * 9 + 5)
                dve.tensor_tensor(cum[:, part_1], cum[:, part_1], moved_late, ALU.add).then_inc(s_latep, 1)
                dve.wait_ge(s_latep, b * 9 + 6)
                dve.tensor_tensor(picked[:, 0, cols], cum[:, cols], mask[:, cols], ALU.mult).then_inc(s_latep, 1)
                dve.wait_ge(s_latep, b * 9 + 7)
                dve.tensor_tensor(rank[:, cols], rank[:, cols], picked[:, 0, cols], ALU.add).then_inc(s_latep, 1)
                dve.tensor_scalar(bucket_l[:, :], bucket_l[:, :], 1.0, None, ALU.add).then_inc(s_latep, 1)
                dve.wait_ge(s_latep, b * 9 + 9)

            def addresses(a, b):
                link(dve.tensor_copy(rank_i[:, a:b], rank[:, a:b]))
                dve.tensor_scalar(rank_p[:, a:b], rank_i[:, a:b], P - 1, None, ALU.bitwise_and)
                link(dve.tensor_scalar(rank_t[:, a:b], rank_i[:, a:b], 7, None, ALU.logical_shift_right))
                link(dve.scalar_tensor_tensor(rank_i[:, a:b], rank_p[:, a:b], float(T), rank_t[:, a:b],
                                              ALU.mult, ALU.add))

            def stage(j, u, batch, staged):
                dve.tensor_copy(stage_addr[:, u, 0:batch], rank_i[:, bass.ds(j, batch)]).then_inc(staged, 1)
                dve.tensor_copy(stage_key[:, u, 0:batch], dst_i[:, bass.ds(j, batch)]).then_inc(staged, 1)

            def stage_early(j, u):
                dve.wait_ge(s_scat[u], j * (16 * BATCH))
                stage(j * (2 * BATCH) + u * BATCH, u, BATCH, s_staged)

            dve.wait_ge(s_rank, BUCKETS)
            addresses(0, NJ_EARLY)
            for u in range(2):
                stage(u * BATCH, u, BATCH, s_staged)
            with dve.Fori(1, BUCKETS // 2 + 1) as j:
                for u in range(2):
                    stage_early(j, u)
                    late_places(j * 2 + (u - 2))
            with dve.Fori(BUCKETS // 2 + 1, NJ_EARLY // (2 * BATCH)) as j:
                for u in range(2):
                    stage_early(j, u)
            addresses(NJ_EARLY, NJ)
            dve.memset(acc[:, :, :], 0.0).then_inc(s_clear, 1)

            def decode(r):
                a, b = TILE[r:r + 2]
                dve.wait_ge(s_skey, 16 * (r + 1))
                dve.tensor_scalar(sdst[:, a:b], skey[:, a:b], 8, None, ALU.logical_shift_right).then_inc(s_place, 1)
                link(dve.tensor_scalar(skey[:, a:b], skey[:, a:b], 255, None, ALU.bitwise_and))
                dve.tensor_copy(splace[:, a:b], skey[:, a:b])
                dve.tensor_copy(splace_b[:, a:b], skey[:, a:b]).then_inc(s_place, 1)
                dve.wait_ge(s_pt, r + 1)
                k, end = a // P, -(-b // P)
                dve.tensor_copy(place_t[:, k:end, :], ps_t[:, 0:end - k, :]).then_inc(s_ptc, 1)

            def compare(g, i, u):
                dve.wait_ge(s_in[u], (i + 1) * 32)
                if not (isinstance(g, int) and g < 2):
                    dve.wait_ge(s_x, g - 1)
                dve.tensor_scalar(pick[:, u % 2, :], place_bc[:, u, :], iota_col[:, 0:1], None,
                                  ALU.is_equal).then_inc(s_pick, 1)

            def relu_low(g, s, c):
                dve.wait_ge(s_hids, g * PAIRS + c + 1)
                dve.scalar_tensor_tensor(hid_lo[:, s, c, :, :].rearrange("p a g -> p (a g)"), ps_a_flat[c], 0.0,
                                         hid_hi[:, s, c, :, :].rearrange("p a g -> p (a g)"),
                                         ALU.max, ALU.subtract).then_inc(s_hid, 1)

            def add_up(g, blk):
                dve.wait_ge(s_seg, g + 1)
                if isinstance(g, int) and g < 1:
                    dve.wait_ge(s_clear, 1)
                else:
                    dve.wait_ge(s_acc, g)
                row = acc[:, bass.ds(blk, 1), :].rearrange("p b r -> p (b r)")
                dve.tensor_tensor(row, row, ps_s[:, 0:VROW], ALU.add).then_inc(s_acc, 1)

            def weights(g, s, u):
                dve.wait_ge(s_expa, g + 1)
                if not (isinstance(g, int) and g < 2):
                    dve.wait_ge(s_vals, g - 1)
                dve.tensor_tensor(vals[:, s, :, VALS:VALS + HEADS], expa[:, s, :, :],
                                  rows[:, u, :, D:HROW].to_broadcast([P, TILES, HEADS]),
                                  ALU.mult).then_inc(s_wgt, 1)

            def weigh(g, s):
                dve.wait_ge(s_wgt, g + 1)
                dve.tensor_tensor(vals[:, s, :, 0:VALS].rearrange("p t (h d) -> p t h d", d=D),
                                  beta[:, s, :, 0:VALS].rearrange("p t (h d) -> p t h d", d=D),
                                  vals[:, s, :, VALS:VALS + HEADS].unsqueeze(3).to_broadcast([P, TILES, HEADS, D]),
                                  ALU.mult).then_inc(s_weighed, 1)

            def low(g, s):
                dve.wait_ge(s_high, g + 1)
                if not (isinstance(g, int) and g < 2):
                    dve.wait_ge(s_seg, g - 1)
                dve.tensor_tensor(vals_lo[:, s, :, :], vals[:, s, :, :], vals_hi[:, s, :, :].bitcast(F32),
                                  ALU.subtract).then_inc(s_vals, 1)

            def leaving(g, s):
                if not (isinstance(g, int) and g < 2):
                    dve.wait_ge(s_seg, g - 1)
                dve.tensor_tensor(leave[:, s, :, :], iota_row[:, :].unsqueeze(1).to_broadcast([P, TILES, P]),
                                  splace[:, bass.ds(g * TILES, TILES)].unsqueeze(2).to_broadcast([P, TILES, P]),
                                  ALU.is_equal).then_inc(s_leave, 1)

            def stage_late(n, slot):
                if not (isinstance(n, int) and n < 1):
                    dve.wait_ge(s_late[slot], n * (16 * LATE_BATCH))
                stage(n * (2 * LATE_BATCH) + (NJ_EARLY + slot * LATE_BATCH), slot, LATE_BATCH, s_lstaged)

            def leaky(g, s):
                dve.wait_ge(s_scaled, g + 1)
                if not (isinstance(g, int) and g < 2):
                    dve.wait_ge(s_weighed, g - 1)
                    dve.wait_ge(s_expa, g - 1)
                dve.tensor_tensor(beta[:, s, :, :], ps_b[:, :, 0:VALS + HEADS], scaled[:, :, :],
                                  ALU.max).then_inc(s_beta, 1)

            def step(r, i, u, done=3, left=4):
                g = i * SLOTS + u
                s = u % 2
                if done > 0:
                    leaky(g - 1, 1 - s)
                late = r < 2
                if late and left > SLOTS and u in (0, 2):
                    stage_late(i - r, u // 2)
                if done > 2:
                    blk = dve.value_load(blk_row[0:1, bass.ds(g - 3, 1)], min_val=0, max_val=BLOCKS)
                if left > 3:
                    compare(g + 3, i + (u + 3) // SLOTS, (u + 3) % SLOTS)
                if done > 2:
                    add_up(g - 3, blk)
                if done > 1:
                    low(g - 2, s)
                if done > 0 and not late:
                    leaving(g - 1, 1 - s)
                if left > 1:
                    relu_low(g + 1, 1 - s, 0)
                if done > 0:
                    weights(g - 1, 1 - s, (u - 1) % SLOTS)
                    if late:
                        weigh(g - 1, 1 - s)
                if left > 1:
                    relu_low(g + 1, 1 - s, 1)
                    relu_low(g + 1, 1 - s, 2)

            def run(r):
                begin, end = RUNS[r:r + 2]
                late = r < 2
                for u in range(3):
                    compare(begin * SLOTS + u, begin, u)
                for c in range(PAIRS):
                    relu_low(begin * SLOTS, 0, c)
                for u in range(SLOTS):
                    step(r, begin, u, done=u, left=SLOTS + 1)
                with dve.Fori(begin + 1, end - 1) as i:
                    for u in range(SLOTS):
                        step(r, i, u, left=SLOTS + 1)
                for u in range(SLOTS):
                    if late and u == 2:
                        decode(r + 1)
                    step(r, end - 1, u, left=SLOTS - u)
                g = end * SLOTS - 1
                blks = [dve.value_load(blk_row[0:1, k:k + 1], min_val=0, max_val=BLOCKS) for k in (g - 2, g - 1, g)]
                leaky(g, 1)
                add_up(g - 2, blks[0])
                low(g - 1, 0)
                if not late:
                    leaving(g, 1)
                weights(g, 1, SLOTS - 1)
                if late:
                    weigh(g, 1)
                low(g, 1)
                add_up(g - 1, blks[1])
                add_up(g, blks[2])

            decode(0)
            for r in range(3):
                run(r)

            mean = stat[:, 0, 0:1]
            dve.tensor_scalar(mean, power[:, 5:6].bitcast(F32), 1.0 / HEADS, None, ALU.mult)
            dve.wait_ge(s_acc, GROUPS)
            sums = acc[:, 0:BLOCKS, VALS:VALS + HEADS]
            link(dve.tensor_scalar(empty[:, :], acc[:, 0:BLOCKS, VROW - 1:VROW].rearrange("p b o -> p (b o)"),
                                   0.0, None, ALU.is_equal))
            link(dve.tensor_tensor(inv[:, 0, :, :], sums, empty[:, :].unsqueeze(2).to_broadcast([P, BLOCKS, HEADS]),
                                   ALU.add))
            link(dve.reciprocal(inv[:, 1, :, :], inv[:, 0, :, :]))
            link(dve.tensor_scalar(inv[:, 2, :, :], inv[:, 1, :, :], 1e-16, None, ALU.add))
            for h in range(HEADS):
                part = acc[:, 0:BLOCKS, h * D:(h + 1) * D]
                link(dve.tensor_tensor(part, part, inv[:, 2, :, h:h + 1].to_broadcast([P, BLOCKS, D]), ALU.mult))
            for h in (0, 2):
                link(dve.tensor_tensor(acc[:, 0:BLOCKS, h * D:(h + 1) * D], acc[:, 0:BLOCKS, h * D:(h + 1) * D],
                                       acc[:, 0:BLOCKS, (h + 1) * D:(h + 2) * D], ALU.add))
            link(dve.tensor_tensor(xc[:, :, :], acc[:, 0:BLOCKS, 0:D], acc[:, 0:BLOCKS, 2 * D:3 * D], ALU.add))
            dve.scalar_tensor_tensor(xc[:, :, :].rearrange("p b d -> p (b d)"),
                                     xc[:, :, :].rearrange("p b d -> p (b d)"),
                                     mean, xs[:, :, :].rearrange("p b d -> p (b d)"),
                                     ALU.mult, ALU.add).then_inc(s_final, 1)

        @block.tensor
        def _(pe):
            pe.wait_ge(s_const, N_CONST)
            pe.wait_ge(s_xin, 16 * N_XIN)
            pe.transpose(ps_pos, pos_rows[:, :], ident[0:64, 0:64]).then_inc(s_wt, 1)
            pe.wait_ge(s_win, 16 * (N_WIN + HEADS))
            for c in range(PAIRS):
                for k in range(2):
                    last = pe.transpose(ps_w[c][:, k, :], w1[:, 2 * c + k, :], ident[:, :])
                last.then_inc(s_wt, 1)
            for k in range(2):
                last = pe.transpose(ps_x[:, 0, k * P:(k + 1) * P], w2[:, k, :], ident[:, :])
            last.then_inc(s_wt, 1)
            pe.wait_ge(s_wmax, 1)
            for h in range(HEADS):
                pe.matmul(ps_b[:, 0, h * D:(h + 1) * D], w1[:, 2 + h, :], w2t[:, h * D:(h + 1) * D],
                          start=True, stop=True)
            for k in range(2):
                last = pe.matmul(ps_b[:, 0, VALS:VALS + HEADS], w1[:, k, :],
                                 w2t[:, VALS + k * HEADS:VALS + (k + 1) * HEADS], start=(k == 0), stop=(k == 1))
            last.then_inc(s_lin, 1)
            pe.wait_ge(s_count, 1)
            pe.matmul(ps_s_bank[:, 0:3 * BUCKETS], before[:, :], count[:, :, :].rearrange("p k b -> p (k b)"),
                      start=True, stop=True)
            pe.matmul(ps_s_bank[:, 3 * BUCKETS:6 * BUCKETS], ones[:, :], count[:, :, :].rearrange("p k b -> p (k b)"),
                      start=True, stop=True).then_inc(s_pref, 1)
            pe.wait_ge(s_past, 1)
            pe.wait_ge(s_wcopy, 1)
            for k in range(2):
                half = slice(k * (GROUPS // 2), (k + 1) * (GROUPS // 2))
                pe.matmul(ps_a_flat[k][:, 0:GROUPS // 2], steps[:, :], iota_group[:, half], start=True, stop=False)
                last = pe.matmul(ps_a_flat[k][:, 0:GROUPS // 2], steps_3[:, :], past_3[:, half],
                                 start=False, stop=True)
            last.then_inc(s_blkp, 1)
            def turn(r):
                pe.wait_ge(s_place, 2 * r + 2)
                k, end = TILE[r] // P, -(-TILE[r + 1] // P)
                for c in range(k, end):
                    last = pe.transpose(ps_t[:, c - k, :], splace_b[:, c * P:(c + 1) * P], ident_b[:, :])
                last.then_inc(s_pt, 1)

            def features(g, i, u):
                pe.wait_ge(s_pick, g + 1)
                pe.wait_ge(s_rows[u], (i + 1) * 32)
                if not (isinstance(g, int) and g < 1):
                    pe.wait_ge(s_feat, g)
                for part in range(2):
                    cols = slice(part * D, (part + 1) * D)
                    pe.matmul(ps_x[0:D, part, :], hblk[:, u, :].bitcast(F16)[:, cols], pick[:, u % 2, :],
                              start=True, stop=True)
                    for t in range(TILES):
                        last = pe.matmul(ps_x[D:P, part, t * P:(t + 1) * P], rows[:, u, t, 0:D].bitcast(F16)[:, cols],
                                         ident_h[:, :],
                                         start=True, stop=True)
                last.then_inc(s_x, 1)

            def layer1(g, f):
                pe.wait_ge(s_feat, g + 1)
                for c in range(PAIRS):
                    if not (isinstance(g, int) and g < 1):
                        pe.wait_ge(s_hid, g * PAIRS + (c - PAIRS + 1))
                    for k in range(2):
                        o = ps_a[c][:, k, :]
                        pe.matmul(o, w1_hi[:, 2 * c + k, :], feat[:, f, 0, :], start=True, stop=False)
                        pe.matmul(o, w1_hi[:, 2 * c + k, :], feat[:, f, 1, :], start=False, stop=False)
                        last = pe.matmul(o, w1_lo[:, 2 * c + k, :], feat[:, f, 0, :], start=False, stop=True)
                    last.then_inc(s_l1, 1)

            def split(o, x_hi, x_lo, w, a, b, stop=False):
                hi, lo = w
                pe.matmul(o, x_hi, hi[:, a:b], start=False, stop=False, skip_group_check=True)
                pe.matmul(o, x_hi, lo[:, a:b], start=False, stop=False, skip_group_check=True)
                return pe.matmul(o, x_lo, hi[:, a:b], start=False, stop=stop, skip_group_check=True)

            def layer2(g, s, f):
                if not (isinstance(g, int) and g < 1):
                    pe.wait_ge(s_beta, g)
                for t in range(TILES):
                    o = ps_b[:, t, 0:VALS + HEADS]
                    cols = slice(t * P, (t + 1) * P)
                    pe.matmul(o, feat[:, f, 0, cols], lin_hi[:, :], start=True, stop=False, skip_group_check=True)
                    pe.matmul(o, feat[:, f, 0, cols], lin_lo[:, :], start=False, stop=False, skip_group_check=True)
                    pe.matmul(o, feat[:, f, 1, cols], lin_hi[:, :], start=False, stop=False, skip_group_check=True)
                pe.wait_ge(s_hid, g * PAIRS + 1)
                for t in range(TILES):
                    cols = slice(t * P, (t + 1) * P)
                    for k in range(2):
                        split(ps_b[:, t, VALS:VALS + HEADS], hid_hi[:, s, 0, k, cols], hid_lo[:, s, 0, k, cols],
                              (w2_hi, w2_lo), VALS + k * HEADS, VALS + (k + 1) * HEADS)
                for h in range(HEADS):
                    if h % 2 == 0:
                        pe.wait_ge(s_hid, g * PAIRS + (h // 2 + 2))
                    for t in range(TILES):
                        cols = slice(t * P, (t + 1) * P)
                        last = split(ps_b[:, t, h * D:(h + 1) * D], hid_hi[:, s, 1 + h // 2, h % 2, cols],
                                     hid_lo[:, s, 1 + h // 2, h % 2, cols], (w2_hi, w2_lo), h * D, (h + 1) * D,
                                     stop=(h == HEADS - 1))
                last.then_inc(s_l2, 1)

            def segment(g, s):
                pe.wait_ge(s_leave, g + 1)
                pe.wait_ge(s_vals, g + 1)
                if not (isinstance(g, int) and g < 1):
                    pe.wait_ge(s_acc, g)
                for t in range(TILES):
                    pe.matmul(ps_s[:, :], leave[:, s, t, :], vals_hi[:, s, t, :], start=(t == 0), stop=False)
                    last = pe.matmul(ps_s[:, :], leave[:, s, t, :], vals_lo[:, s, t, :],
                                     start=False, stop=(t == TILES - 1))
                last.then_inc(s_seg, 1)

            def step(i, u, left=3, done=2):
                g = i * SLOTS + u
                if left > 2:
                    features(g + 2, i + (u + 2) // SLOTS, (u + 2) % SLOTS)
                if left > 1:
                    layer1(g + 1, (u + 1) % 3)
                layer2(g, u % 2, u % 3)
                if done > 1:
                    segment(g - 2, u % 2)

            def run(r):
                begin, end = RUNS[r:r + 2]
                g = begin * SLOTS
                features(g, begin, 0)
                features(g + 1, begin, 1)
                layer1(g, 0)
                for u in range(SLOTS):
                    step(begin, u, done=u)
                with pe.Fori(begin + 1, end - 1) as i:
                    for u in range(SLOTS):
                        step(i, u)
                for u in range(SLOTS):
                    if r < 2 and u == 2:
                        turn(r + 1)
                    step(end - 1, u, left=SLOTS - u)
                segment(end * SLOTS - 2, 0)
                segment(end * SLOTS - 1, 1)

            turn(0)
            for r in range(3):
                run(r)


_INS = ['x', 'src', 'dst', 'node_vec', 'L0_gnn_gate_w1', 'L0_gnn_gate_w2', 'L0_gnn_msg_w1', 'L0_gnn_msg_w2']
_OUTS = [((6250, 64), 'float32')]


def kernel(**inputs):
    import numpy as _np
    import concourse.bacc as _bacc
    from concourse import mybir as _mybir
    from concourse.bass_utils import run_bass_kernel_spmd as _run

    nc = _bacc.Bacc("TRN2", target_bir_lowering=False, num_devices=1)
    arrays, args = {}, []
    for name in _INS:
        a = _np.ascontiguousarray(inputs[name])
        arrays[f"in_{name}_dram"] = a
        args.append(nc.dram_tensor(f"in_{name}_dram", a.shape, _mybir.dt.from_np(a.dtype), kind="ExternalInput").ap())
    for i, (shape, dtype) in enumerate(_OUTS):
        dt = _mybir.dt.from_np(_np.dtype(dtype))
        args.append(nc.dram_tensor(f"out_{i}_dram", shape, dt, kind="ExternalOutput").ap())
    gnn_preln_kernel(nc, *args)
    r = _run(nc, [arrays], core_ids=[0])
    got = tuple(r.results[0][f"out_{i}_dram"] for i in range(len(_OUTS)))
    return got[0]
```
